# Optimizing a Trainium2 kernel written in Bass

```python
import numpy as np
import jax
import jax.numpy as jnp

def _softmax(x, axis=-1):
    return jax.nn.softmax(x, axis=axis)

def _gelu(x):
    return jax.nn.gelu(x, approximate=True)

def _silu(x):
    return jax.nn.silu(x)

def _sigmoid(x):
    return jax.nn.sigmoid(x)

def _layernorm(x, axis=-1, eps=1e-05):
    m = jnp.mean(x, axis=axis, keepdims=True)
    v = jnp.var(x, axis=axis, keepdims=True)
    return (x - m) / jnp.sqrt(v + eps)

def _scatter_add(tgt, idx, src, axis=0):
    return tgt.at[idx].add(src)

def _segment_sum(src, seg, n):
    return jax.ops.segment_sum(src, seg, n)
kernel_name = 'mk_lm_tower_d1_tok_ids1024_r4_052157'

def setup_inputs(seed: int=0):
    np.random.seed(seed)
    _w = jnp.asarray

    def _rec_inputs():
        import jax
        import jax.numpy as jnp
        _rk = jax.random.key(seed)
        x = jax.random.randint(jax.random.fold_in(_rk, 1), (2, 2048), 0, 12564, jnp.int32)
        return x
    x = _rec_inputs()

    def _L0_tok_setup():
        import jax, jax.numpy as jnp
        import numpy as np
        B, T, D, INNER, N, V, L, P = (4, 1024, 256, 512, 64, 50257, 4, 5000)
        DECAY, INP = (0.95, 0.05)

        def _silu(x):
            return x * jax.nn.sigmoid(x)

        def _layer(x, W_in_l, cw, cb, WB, WC, Dv, Wo, g, b):
            xp = x @ W_in_l.T
            x_in, x_gate = jnp.split(xp, 2, axis=-1)
            xc = jnp.transpose(x_in, (0, 2, 1))
            xc = jnp.pad(xc, ((0, 0), (0, 0), (3, 0)))
            xc = jax.lax.conv_general_dilated(xc, cw, window_strides=(1,), padding='VALID', dimension_numbers=('NCH', 'OIH', 'NCH'), feature_group_count=INNER)
            xc = xc + cb[None, :, None]
            u = _silu(jnp.transpose(xc, (0, 2, 1)))
            Bu = u @ WB.T

            def step(h, bu):
                h = DECAY * h + INP * bu
                return (h, h)
            h0 = jnp.zeros((x.shape[0], Bu.shape[-1]), x.dtype)
            _, hs = jax.lax.scan(step, h0, jnp.swapaxes(Bu, 0, 1))
            hs = jnp.swapaxes(hs, 0, 1)
            y = hs @ WC.T + Dv * u
            y = y * _silu(x_gate)
            y = y @ Wo.T
            z = y + x
            mu = jnp.mean(z, axis=-1, keepdims=True)
            var = jnp.var(z, axis=-1, keepdims=True)
            return (z - mu) * jax.lax.rsqrt(var + 1e-05) * g + b
        key = jax.random.key(seed)
        ks = jax.random.split(key, 10)
        s = 0.02
        return {'tokens': jax.random.randint(ks[0], (B, T), 0, V), 'tok_emb': jax.random.normal(ks[1], (V, D), jnp.float32) * s, 'pos_emb': jax.random.normal(ks[2], (P, D), jnp.float32) * s, 'W_in': jax.random.normal(ks[3], (L, 2 * INNER, D), jnp.float32) * s, 'conv_w': jax.random.normal(ks[4], (L, INNER, 1, 4), jnp.float32) * s, 'conv_b': jnp.zeros((L, INNER), jnp.float32), 'W_B': jax.random.normal(ks[5], (L, N, INNER), jnp.float32) * s, 'W_C': jax.random.normal(ks[6], (L, INNER, N), jnp.float32) * s, 'D_vec': jax.random.normal(ks[7], (L, INNER), jnp.float32) * s, 'W_out': jax.random.normal(ks[8], (L, D, INNER), jnp.float32) * s, 'ln_g': jnp.ones((L, D), jnp.float32), 'ln_b': jnp.zeros((L, D), jnp.float32)}
    _L0_tok_all = _L0_tok_setup()
    _L0_tok_in = {k: v for k, v in _L0_tok_all.items() if k in ('tok_emb', 'pos_emb', 'W_in', 'conv_w', 'conv_b', 'W_B', 'W_C', 'D_vec', 'W_out', 'ln_g', 'ln_b')}
    del _L0_tok_all

    def _L0_attn_setup():
        import jax, jax.numpy as jnp
        import numpy as np
        B, T, C = (64, 64, 256)
        N_HEAD, HEAD_SIZE, KV_RANK = (16, 64, 128)
        BLOCK_SIZE = 64
        key = jax.random.key(seed)
        ks = jax.random.split(key, 5)
        HD = N_HEAD * HEAD_SIZE

        def init(k, shape):
            fan_in = shape[0]
            bound = 1.0 / np.sqrt(fan_in)
            return jax.random.uniform(k, shape, jnp.float32, -bound, bound)
        return {'x': jax.random.normal(ks[0], (B, T, C), jnp.float32), 'w_kv_down': init(ks[1], (C, KV_RANK)), 'w_kv_up': init(ks[2], (KV_RANK, 2 * HD)), 'w_q': init(ks[3], (C, HD)), 'w_out': init(ks[4], (HD, C))}
    _L0_attn_all = _L0_attn_setup()
    _L0_attn_in = {k: v for k, v in _L0_attn_all.items() if k in ('w_kv_down', 'w_kv_up', 'w_q', 'w_out')}
    del _L0_attn_all

    def _L0_ffn_setup():
        import jax, jax.numpy as jnp
        import numpy as np
        B, S, H = (4, 512, 256)
        E = 8
        GS = 2
        NG = E // GS
        F = int(H * 4 * (2.0 / 3.0))
        key = jax.random.key(seed)
        ks = jax.random.split(key, 7)
        sc_h = 1.0 / np.sqrt(H)
        sc_f = 1.0 / np.sqrt(F)
        return {'x': jax.random.normal(ks[0], (B, S, H), dtype=jnp.float32), 'Wr': jax.random.normal(ks[1], (H, E), dtype=jnp.float32) * sc_h, 'br': jnp.zeros((E,), dtype=jnp.float32), 'W_up': jax.random.normal(ks[2], (NG, H, F), dtype=jnp.float32) * sc_h, 'b_up': jax.random.normal(ks[3], (NG, F), dtype=jnp.float32) * 0.01, 'W_down': jax.random.normal(ks[4], (E, F, H), dtype=jnp.float32) * sc_f, 'b_down': jax.random.normal(ks[5], (E, H), dtype=jnp.float32) * 0.01}
    _L0_ffn_all = _L0_ffn_setup()
    _L0_ffn_in = {k: v for k, v in _L0_ffn_all.items() if k in ('Wr', 'br', 'W_up', 'b_up', 'W_down', 'b_down')}
    del _L0_ffn_all
    return {'x': x, 'L0_tok_tok_emb': _L0_tok_in['tok_emb'], 'L0_tok_pos_emb': _L0_tok_in['pos_emb'], 'L0_tok_W_in': _L0_tok_in['W_in'], 'L0_tok_conv_w': _L0_tok_in['conv_w'], 'L0_tok_conv_b': _L0_tok_in['conv_b'], 'L0_tok_W_B': _L0_tok_in['W_B'], 'L0_tok_W_C': _L0_tok_in['W_C'], 'L0_tok_D_vec': _L0_tok_in['D_vec'], 'L0_tok_W_out': _L0_tok_in['W_out'], 'L0_tok_ln_g': _L0_tok_in['ln_g'], 'L0_tok_ln_b': _L0_tok_in['ln_b'], 'L0_attn_w_kv_down': _L0_attn_in['w_kv_down'], 'L0_attn_w_kv_up': _L0_attn_in['w_kv_up'], 'L0_attn_w_q': _L0_attn_in['w_q'], 'L0_attn_w_out': _L0_attn_in['w_out'], 'L0_ffn_Wr': _L0_ffn_in['Wr'], 'L0_ffn_br': _L0_ffn_in['br'], 'L0_ffn_W_up': _L0_ffn_in['W_up'], 'L0_ffn_b_up': _L0_ffn_in['b_up'], 'L0_ffn_W_down': _L0_ffn_in['W_down'], 'L0_ffn_b_down': _L0_ffn_in['b_down']}

def reference(x, L0_tok_tok_emb, L0_tok_pos_emb, L0_tok_W_in, L0_tok_conv_w, L0_tok_conv_b, L0_tok_W_B, L0_tok_W_C, L0_tok_D_vec, L0_tok_W_out, L0_tok_ln_g, L0_tok_ln_b, L0_attn_w_kv_down, L0_attn_w_kv_up, L0_attn_w_q, L0_attn_w_out, L0_ffn_Wr, L0_ffn_br, L0_ffn_W_up, L0_ffn_b_up, L0_ffn_W_down, L0_ffn_b_down):
    import jax
    import jax.numpy as jnp

    def _L0_tok_ref(tokens, tok_emb, pos_emb, W_in, conv_w, conv_b, W_B, W_C, D_vec, W_out, ln_g, ln_b):
        import jax, jax.numpy as jnp
        import numpy as np
        B, T, D, INNER, N, V, L, P = (4, 1024, 256, 512, 64, 50257, 4, 5000)
        DECAY, INP = (0.95, 0.05)

        def _silu(x):
            return x * jax.nn.sigmoid(x)

        def _layer(x, W_in_l, cw, cb, WB, WC, Dv, Wo, g, b):
            xp = x @ W_in_l.T
            x_in, x_gate = jnp.split(xp, 2, axis=-1)
            xc = jnp.transpose(x_in, (0, 2, 1))
            xc = jnp.pad(xc, ((0, 0), (0, 0), (3, 0)))
            xc = jax.lax.conv_general_dilated(xc, cw, window_strides=(1,), padding='VALID', dimension_numbers=('NCH', 'OIH', 'NCH'), feature_group_count=INNER)
            xc = xc + cb[None, :, None]
            u = _silu(jnp.transpose(xc, (0, 2, 1)))
            Bu = u @ WB.T

            def step(h, bu):
                h = DECAY * h + INP * bu
                return (h, h)
            h0 = jnp.zeros((x.shape[0], Bu.shape[-1]), x.dtype)
            _, hs = jax.lax.scan(step, h0, jnp.swapaxes(Bu, 0, 1))
            hs = jnp.swapaxes(hs, 0, 1)
            y = hs @ WC.T + Dv * u
            y = y * _silu(x_gate)
            y = y @ Wo.T
            z = y + x
            mu = jnp.mean(z, axis=-1, keepdims=True)
            var = jnp.var(z, axis=-1, keepdims=True)
            return (z - mu) * jax.lax.rsqrt(var + 1e-05) * g + b
        x = tok_emb[tokens] + pos_emb[jnp.arange(tokens.shape[1])][None]
        for l in range(L):
            x = _layer(x, W_in[l], conv_w[l], conv_b[l], W_B[l], W_C[l], D_vec[l], W_out[l], ln_g[l], ln_b[l])
        return x

    def _L0_attn_ref(x, w_kv_down, w_kv_up, w_q, w_out):
        import jax, jax.numpy as jnp
        import numpy as np
        B, T, C = (64, 64, 256)
        N_HEAD, HEAD_SIZE, KV_RANK = (16, 64, 128)
        BLOCK_SIZE = 64
        Bx, Tx, Cx = x.shape
        HD = N_HEAD * HEAD_SIZE
        latent_kv = x @ w_kv_down
        kv = latent_kv @ w_kv_up
        k, v = (kv[..., :HD], kv[..., HD:])
        k = k.reshape(Bx, Tx, N_HEAD, HEAD_SIZE)
        v = v.reshape(Bx, Tx, N_HEAD, HEAD_SIZE)
        q = (x @ w_q).reshape(Bx, Tx, N_HEAD, HEAD_SIZE)
        scale = HEAD_SIZE ** (-0.5)
        att = jnp.einsum('bqhd,bkhd->bhqk', q, k) * scale
        causal = jnp.tril(jnp.ones((Tx, Tx), dtype=bool))
        att = jnp.where(causal, att, -jnp.inf)
        att = jax.nn.softmax(att, axis=-1)
        y = jnp.einsum('bhqk,bkhd->bqhd', att, v)
        y = y.reshape(Bx, Tx, HD)
        return y @ w_out

    def _L0_ffn_ref(x, Wr, br, W_up, b_up, W_down, b_down):
        import jax, jax.numpy as jnp
        import numpy as np
        B, S, H = (4, 512, 256)
        E = 8
        GS = 2
        NG = E // GS
        F = int(H * 4 * (2.0 / 3.0))
        b, s, h = x.shape
        n_tok = b * s
        k = n_tok // E
        xf = x.reshape(n_tok, h)
        logits = xf @ Wr + br
        Sm = jax.nn.softmax(logits, axis=-1)
        G_t, idx_t = jax.lax.top_k(Sm.T, k)
        G = G_t.T
        idx = idx_t.T
        tokens = xf[idx]
        group = jnp.arange(E) // GS
        Wu = W_up[group]
        bu = b_up[group]
        mid = jax.nn.silu(jnp.einsum('keh,ehf->kef', tokens, Wu) + bu)
        out = jnp.einsum('kef,efh->keh', mid, W_down) + b_down
        y = jnp.zeros_like(xf).at[idx].add(G[..., None] * out)
        return y.reshape(b, s, h)
    h = _L0_tok_ref(x, L0_tok_tok_emb, L0_tok_pos_emb, L0_tok_W_in, L0_tok_conv_w, L0_tok_conv_b, L0_tok_W_B, L0_tok_W_C, L0_tok_D_vec, L0_tok_W_out, L0_tok_ln_g, L0_tok_ln_b)
    h = h + _L0_attn_ref(_layernorm(h, axis=-1), L0_attn_w_kv_down, L0_attn_w_kv_up, L0_attn_w_q, L0_attn_w_out)
    h = h + _L0_ffn_ref(_layernorm(h, axis=-1), L0_ffn_Wr, L0_ffn_br, L0_ffn_W_up, L0_ffn_b_up, L0_ffn_W_down, L0_ffn_b_down)
    return h

_drawn_inputs = setup_inputs


def setup_inputs(seed=0):
    import zlib

    import numpy as np

    out = dict(_drawn_inputs(seed))
    spreads = {'L0_tok_conv_b': (0.0, 0.8),
     'L0_tok_ln_g': (1.0, 0.2),
     'L0_tok_ln_b': (0.0, 0.1),
     'L0_ffn_br': (0.0, 0.1)}
    factors = {'L0_tok_W_in': 8.0,
     'L0_tok_conv_w': 8.0,
     'L0_tok_W_B': 8.0,
     'L0_tok_W_C': 8.0,
     'L0_tok_D_vec': 8.0,
     'L0_tok_W_out': 8.0,
     'L0_attn_w_q': 4.94,
     'L0_ffn_b_up': 31.165,
     'L0_ffn_b_down': 8.0}
    for name, (base, spread) in spreads.items():
        noise = np.random.default_rng([zlib.crc32(name.encode()), seed]).standard_normal(out[name].shape)
        drawn = base * np.exp(spread * noise) if base else spread * noise
        out[name] = jnp.asarray(drawn.astype(out[name].dtype))
    for name, factor in factors.items():
        out[name] = (out[name] * factor).astype(out[name].dtype)
    return out
```

```python
from contextlib import ExitStack

import concourse.bass as bass
from concourse import mybir

P = 128
F32 = mybir.dt.float32
F32R = mybir.dt.float32r
BF16 = mybir.dt.bfloat16
F16 = mybir.dt.float16
I32 = mybir.dt.int32
U32 = mybir.dt.uint32
ALU = mybir.AluOpType
ACT = mybir.ActivationFunctionType
AX = mybir.AxisListType

LN_EPS = 1e-5


class Event:

    def __init__(self, sem, per_round, before=0):
        self.sem, self.per_round, self.start = sem, per_round, per_round - before

    def at(self, rnd, count):
        return (rnd + 1) * self.per_round + count


def build_token_mixer(nc, d, h_out):
    B, T = d["x"].shape[1], d["x"].shape[2] * P
    _, L, KC, TWO_INNER = d["w_in"].shape
    D = KC * P
    INNER = TWO_INNER // 2
    IC = INNER // P
    N = d["w_b"].shape[3]
    TAPS = d["conv_w"].shape[3]
    BLK = 512
    TB = BLK // P
    ROUNDS = T // BLK
    UNITS = L * B
    DECAY, INP = 0.95, 0.05
    HALO = TAPS - 1
    A_RING, C_RING, D_RING = 4, 2, 2

    GATES, TURNED = IC, 2 * IC
    A_PER = 2 * IC + KC
    C_PER, D_PER = IC + 1, TB // 2
    STAT_PER = 2 * TB + 1
    assert (UNITS * A_PER) % A_RING == 0 and (UNITS * C_PER) % C_RING == 0 and D_PER % D_RING == 0

    with ExitStack() as ctx:
        def sb(name, shape, dt=F32):
            return ctx.enter_context(nc.sbuf_tensor(name, shape, dt))

        def sem(name):
            return ctx.enter_context(nc.semaphore(name))

        def event(name, per_round, before=0):
            return Event(sem(name), per_round, before)

        w_in = sb("tm_w_in", [P, L, KC, TWO_INNER])
        w_b = sb("tm_w_b", [P, L, IC, P])
        w_c = sb("tm_w_c", [P, L, INNER])
        w_out = sb("tm_w_out", [P, L, IC, D])
        conv_w = sb("tm_conv_w", [P, L, IC, TAPS])
        conv_b = sb("tm_conv_b", [P, L, IC])
        d_vec = sb("tm_d_vec", [P, L, IC])
        g_col = sb("tm_g_col", [P, L, KC])
        b_col = sb("tm_b_col", [P, L, KC])
        g_row = sb("tm_g_row", [P, L, D])
        b_row = sb("tm_b_row", [P, L, D])
        ident = sb("tm_ident", [P, P])
        decay = sb("tm_decay", [P, BLK])
        minus_half = sb("tm_minus_half", [P, TB])
        ids = sb("tm_ids", [P, B, ROUNDS * TB], I32)
        ids_now = sb("tm_ids_now", [P, B * TB], I32)
        emb = sb("tm_emb", [P, B * TB, D])
        pos = sb("tm_pos", [P, TB, D])
        resid = [sb(f"tm_resid{b}", [P, TB, D]) for b in range(B)]
        done = [sb(f"tm_done{b}", [P, TB, D]) for b in range(B)]
        x_t = [sb(f"tm_x_t{b}", [P, KC, BLK]) for b in range(B)]
        xin = [sb(f"tm_xin{i}", [P, IC, HALO + BLK]) for i in range(2)]
        act_u = [sb(f"tm_u{i}", [P, IC, BLK]) for i in range(2)]
        gate = [sb(f"tm_gate{i}", [P, IC, BLK]) for i in range(2)]
        y = sb("tm_y", [P, IC, BLK])
        bu = sb("tm_bu", [P, BLK])
        hs = sb("tm_hs", [P, BLK])
        z = sb("tm_z", [P, TB, D])
        z_hat = sb("tm_z_hat", [P, TB, D])
        stats = sb("tm_stats", [P, TB, 6])
        mean_var = sb("tm_mean_var", [P, TB, 2])
        var_eps = sb("tm_var_eps", [P, TB])
        rstd = sb("tm_rstd", [P, TB])
        conv_tail = sb("tm_conv_tail", [P, UNITS, IC, HALO])
        state_tail = sb("tm_state_tail", [P, UNITS])
        ring_a = [ctx.enter_context(nc.psum_tensor(f"tm_ring_a{i}", [P, BLK], F32)) for i in range(A_RING)]
        ring_c = [ctx.enter_context(nc.psum_tensor(f"tm_ring_c{i}", [P, BLK], F32)) for i in range(C_RING)]
        ring_d = [ctx.enter_context(nc.psum_tensor(f"tm_ring_d{i}", [P, 2, D], F32)) for i in range(D_RING)]

        w_in_in = [sem(f"tm_w_in_in{l}") for l in range(L)]
        w_b_in = sem("tm_w_b_in")
        w_c_in = sem("tm_w_c_in")
        w_out_in = sem("tm_w_out_in")
        columns_in = sem("tm_columns_in")
        norm_rows_in = sem("tm_norm_rows_in")
        ids_in = sem("tm_ids_in")
        set_up = sem("tm_set_up")
        tails_zero = sem("tm_tails_zero")
        ident_zero = sem("tm_ident_zero")
        gather_begun = sem("tm_gather_begun")
        aggregation_begun = sem("tm_aggregation_begun")
        ids_staged = sem("tm_ids_staged")
        emb_in = sem("tm_emb_in")
        pos_in = sem("tm_pos_in")
        emb_added = event("tm_emb_added", 2 * B, 2)
        a_full = event("tm_a_full", UNITS * A_PER, KC)
        c_full = event("tm_c_full", UNITS * C_PER)
        d_full = event("tm_d_full", UNITS * D_PER)
        a_drained = event("tm_a_drained", UNITS * A_PER, KC)
        c_drained = event("tm_c_drained", UNITS * C_PER)
        d_drained = event("tm_d_drained", UNITS * D_PER)
        halo_in = event("tm_halo_in", UNITS)
        conv_step = event("tm_conv_step", UNITS * IC * TAPS)
        tail_kept = event("tm_tail_kept", UNITS)
        u_ready = event("tm_u_ready", UNITS * IC)
        scanned = event("tm_scanned", UNITS)
        stat_step = event("tm_stat_step", UNITS * STAT_PER)
        rstd_ready = event("tm_rstd_ready", UNITS)
        z_hat_ready = event("tm_z_hat_ready", UNITS * TB)
        y_ready = event("tm_y_ready", UNITS * IC)
        scaled = event("tm_scaled", UNITS * TB)
        rows_ready = event("tm_rows_ready", UNITS * TB)
        stored = [event(f"tm_stored{b}", 16) for b in range(B)]

        def place(u):
            return (u % UNITS) // B, u % B

        def run(eng, unit, finish):
            for u in range(UNITS):
                unit(0, u, True, False)
            with eng.Fori(1, ROUNDS - 1) as rnd:
                for u in range(UNITS):
                    unit(rnd, u, False, False)
            for u in range(UNITS):
                unit(ROUNDS - 1, u, False, True)
            finish(ROUNDS, -1)

        block = ctx.enter_context(nc.Block())

        @block.sync
        def _(sp):
            for ev in stored:
                sp.sem_inc(ev.sem, ev.start)

            def load_positions(rnd):
                sp.dma_start(pos[:], d["pos_emb"][bass.ds(rnd * BLK, BLK), :]
                             .rearrange("(t p) n -> p t n", p=P)).then_inc(pos_in, 16)

            def store(rnd, u):
                b = place(u)[1]
                block_of = rnd if u >= 0 else rnd - 1
                sp.wait_ge(rows_ready.sem, rows_ready.at(rnd, (u + 1) * TB))
                sp.dma_start(h_out[bass.ds(block_of * BLK + b * T, BLK), :].rearrange("(t p) n -> p t n", p=P),
                             done[b][:]).then_inc(stored[b].sem, 16)

            sp.dma_start(ids[:], d["x"]).then_inc(ids_in, 16)
            load_positions(0)
            sp.dma_start(w_in[:, 0], d["w_in"][:, 0]).then_inc(w_in_in[0], 16)
            sp.wait_ge(emb_added.sem, emb_added.at(0, 0))
            sp.dma_start(w_b[:, :, :, 0:N], d["w_b"]).then_inc(w_b_in, 16)
            sp.dma_start(w_c[0:N], d["w_c"]).then_inc(w_c_in, 16)
            sp.dma_start(w_out[:], d["w_out"]).then_inc(w_out_in, 16)
            sp.dma_start(g_row[:], d["ln_g"].partition_broadcast(P)).then_inc(norm_rows_in, 16)
            sp.dma_start(b_row[:], d["ln_b"].partition_broadcast(P)).then_inc(norm_rows_in, 16)
            for l in range(1, L):
                sp.dma_start(w_in[:, l], d["w_in"][:, l]).then_inc(w_in_in[l], 16)

            def unit(rnd, u, first, last):
                if u == 0 and not last:
                    sp.wait_ge(emb_added.sem, emb_added.at(rnd, 2))
                    load_positions(rnd + 1)
                if u - 1 == UNITS - B or (u == 0 and not first):
                    store(rnd, u - 1)

            run(sp, unit, store)
            for ev in stored:
                sp.wait_ge(ev.sem, ev.at(ROUNDS - 1, 16))

        @block.gpsimd
        def _(pool):
            for ev in (rstd_ready, y_ready, scaled, rows_ready):
                pool.sem_inc(ev.sem, ev.start)

            def gather(rnd):
                pool.tensor_copy(ids_now[:].rearrange("p (b t) -> p b t", b=B),
                                 ids[:, :, bass.ds(rnd * TB, TB)]).then_inc(ids_staged, 1)
                pool.wait_ge(ids_staged, rnd + 1)
                pool.sem_inc(gather_begun, 1)
                for i in range(B * TB):
                    pool.indirect_dma_start(
                        out=emb[:, i, :], out_offset=None, in_=d["tok_emb"],
                        in_offset=bass.IndirectOffsetOnAxis(ap=ids_now[:, i:i + 1], axis=0),
                    ).then_inc(emb_in, 16)

            pool.memset(ident[:], 0.0).then_inc(ident_zero, 1)
            pool.memset(decay[:], DECAY).then_inc(set_up, 1)
            pool.memset(minus_half[:], -0.5).then_inc(set_up, 1)
            pool.wait_ge(ident_zero, 1)
            pool.affine_select(out=ident[:], in_=ident[:], compare_op=ALU.not_equal, fill=1.0, base=0,
                               pattern=[[-1, P]], channel_multiplier=1).then_inc(set_up, 1)
            pool.wait_ge(ids_in, 16)
            gather(0)
            pool.wait_ge(set_up, 3)
            pool.wait_ge(norm_rows_in, 32)

            def norm_rows(rnd, u):
                l, b = place(u)
                pool.wait_ge(stat_step.sem, stat_step.at(rnd, (u + 1) * STAT_PER))
                pool.tensor_tensor(rstd[:], var_eps[:], minus_half[:], ALU.pow).then_inc(rstd_ready.sem, 1)
                rows = resid[b] if l < L - 1 else done[b]
                if l == L - 1:
                    pool.wait_ge(stored[b].sem, stored[b].at(rnd if u >= 0 else rnd - 1, 0))
                else:
                    pool.wait_ge(d_drained.sem, d_drained.at(rnd, (u + 1) * D_PER))
                for t in range(TB):
                    pool.wait_ge(z_hat_ready.sem, z_hat_ready.at(rnd, u * TB + t + 1))
                    pool.tensor_tensor(rows[:, t, :], z_hat[:, t, :], g_row[:, l, :],
                                       ALU.mult).then_inc(scaled.sem, 1)
                for t in range(TB):
                    pool.wait_ge(scaled.sem, scaled.at(rnd, u * TB + t + 1))
                    pool.tensor_tensor(rows[:, t, :], rows[:, t, :], b_row[:, l, :],
                                       ALU.add).then_inc(rows_ready.sem, 1)

            def unit(rnd, u, first, last):
                if u >= 1 or not first:
                    norm_rows(rnd, u - 1)
                for c in range(IC):
                    pool.wait_ge(c_drained.sem, c_drained.at(rnd, u * C_PER + c + 2))
                    pool.wait_ge(a_drained.sem, a_drained.at(rnd, u * A_PER + GATES + c + 1))
                    pool.tensor_tensor(y[:, c, :], y[:, c, :], gate[u % 2][:, c, :],
                                       ALU.mult).then_inc(y_ready.sem, 1)
                if u == 1 and not last:
                    pool.wait_ge(emb_added.sem, emb_added.at(rnd, 2))
                    gather(rnd + 1)

            run(pool, unit, norm_rows)

        @block.scalar
        def _(act):
            for ev in (a_drained, u_ready):
                act.sem_inc(ev.sem, ev.start)
            act.dma_start(conv_w[:], d["conv_w"]).then_inc(columns_in, 16)
            act.dma_start(conv_b[:], d["conv_b"]).then_inc(columns_in, 16)
            act.dma_start(d_vec[:], d["d_vec"]).then_inc(columns_in, 16)
            act.dma_start(g_col[:], d["g_col"]).then_inc(columns_in, 16)
            act.dma_start(b_col[:], d["b_col"]).then_inc(columns_in, 16)

            def take(rnd, n, out, func=ACT.Copy, **kw):
                act.wait_ge(a_full.sem, a_full.at(rnd, n + 1))
                act.activation(out, ring_a[n % A_RING][:], func, **kw).then_inc(a_drained.sem, 1)

            def unit(rnd, u, first, last):
                l, b = place(u)
                par, n = u % 2, u * A_PER
                act.wait_ge(conv_step.sem, conv_step.at(rnd, (u - 1) * IC * TAPS))
                act.wait_ge(tail_kept.sem, tail_kept.at(rnd, u - 1))
                for c in range(IC):
                    take(rnd, n + c, xin[par][:, c, HALO:])
                for c in range(IC):
                    act.wait_ge(conv_step.sem, conv_step.at(rnd, (u * IC + c + 1) * TAPS))
                    act.activation(act_u[par][:, c, :], act_u[par][:, c, :], ACT.Silu,
                                   bias=conv_b[:, l, c:c + 1]).then_inc(u_ready.sem, 1)
                act.wait_ge(y_ready.sem, y_ready.at(rnd, (u - 1) * IC))
                for c in range(IC):
                    take(rnd, n + GATES + c, gate[par][:, c, :], ACT.Silu)
                if u == UNITS - 1 and last:
                    return
                for k in range(KC):
                    if u == 0 or u == UNITS - 1:
                        take(rnd, n + TURNED + k, x_t[1 - b][:, k, :])
                    else:
                        pl = (u - 1) // B
                        take(rnd, n + TURNED + k, x_t[1 - b][:, k, :], ACT.Identity,
                             scale=g_col[:, pl, k:k + 1], bias=b_col[:, pl, k:k + 1])

            for k in range(KC):
                take(0, k - KC, x_t[0][:, k, :])
            act.wait_ge(columns_in, 16 * 5)
            run(act, unit, lambda rnd, u: None)

        @block.vector
        def _(dve):
            for ev in (emb_added, c_drained, d_drained, halo_in, conv_step, tail_kept, scanned,
                       stat_step, z_hat_ready):
                dve.sem_inc(ev.sem, ev.start)
            dve.memset(conv_tail[:], 0.0).then_inc(tails_zero, 1)
            dve.memset(state_tail[:], 0.0).then_inc(tails_zero, 1)
            dve.memset(w_b[:, :, :, N:], 0.0).then_inc(tails_zero, 1)
            dve.memset(w_c[N:], 0.0).then_inc(tails_zero, 1)

            def embed(rnd, b):
                dve.wait_ge(pos_in, (rnd + 1) * 16)
                dve.wait_ge(emb_in, (rnd + 1) * (16 * B * TB))
                for i in range(2):
                    s = slice(i * TB // 2, (i + 1) * TB // 2)
                    se = slice(b * TB + i * TB // 2, b * TB + (i + 1) * TB // 2)
                    dve.tensor_tensor(resid[b][:, s, :], emb[:, se, :], pos[:, s, :],
                                      ALU.add).then_inc(emb_added.sem, 1)

            def convolve(rnd, u):
                l, par = u // B, u % 2
                dve.tensor_copy(xin[par][:, :, 0:HALO], conv_tail[:, u]).then_inc(halo_in.sem, 1)
                dve.wait_ge(halo_in.sem, halo_in.at(rnd, u + 1))
                for c in range(IC):
                    dve.wait_ge(a_drained.sem, a_drained.at(rnd, u * A_PER + c + 1))
                    if c == 0:
                        dve.wait_ge(c_full.sem, c_full.at(rnd, (u - 1) * C_PER))
                    acc = act_u[par][:, c, :]
                    for j in range(TAPS):
                        src = xin[par][:, c, j:j + BLK]
                        if j == 0:
                            i = dve.tensor_scalar(acc, src, conv_w[:, l, c, 0:1], None, ALU.mult)
                        else:
                            dve.wait_ge(conv_step.sem, conv_step.at(rnd, (u * IC + c) * TAPS + j))
                            i = dve.scalar_tensor_tensor(out=acc, in0=src, scalar=conv_w[:, l, c, j:j + 1],
                                                         in1=acc, op0=ALU.mult, op1=ALU.add)
                        i.then_inc(conv_step.sem, 1)
                dve.tensor_copy(conv_tail[:, u], xin[par][:, :, BLK:]).then_inc(tail_kept.sem, 1)

            def recur(rnd, u):
                n = u * C_PER
                dve.wait_ge(c_full.sem, c_full.at(rnd, n + 1))
                dve.tensor_scalar(bu[:], ring_c[n % C_RING][:], INP, None, ALU.mult).then_inc(c_drained.sem, 1)
                dve.wait_ge(c_drained.sem, c_drained.at(rnd, n + 1))
                dve.tensor_tensor_scan(hs[:], decay[:], bu[:], state_tail[:, u:u + 1], ALU.mult,
                                       ALU.add).then_inc(scanned.sem, 1)
                dve.wait_ge(scanned.sem, scanned.at(rnd, u + 1))
                dve.tensor_copy(state_tail[:, u:u + 1], hs[:, BLK - 1:])

            def row_stats(rnd, u):
                b = place(u)[1]
                for i in range(D_PER):
                    n = u * D_PER + i
                    dve.wait_ge(d_full.sem, d_full.at(rnd, n + 1))
                    if u in range(B):
                        dve.wait_ge(emb_added.sem, emb_added.at(rnd, 2 * b))
                    else:
                        dve.wait_ge(rows_ready.sem, rows_ready.at(rnd, (u - B) * TB + 2 * i + 2))
                    dve.tensor_tensor(z[:, 2 * i:2 * i + 2, :], ring_d[n % D_RING][:],
                                      resid[b][:, 2 * i:2 * i + 2, :], ALU.add).then_inc(d_drained.sem, 1)
                for t in range(TB):
                    dve.wait_ge(d_drained.sem, d_drained.at(rnd, u * D_PER + t // 2 + 1))
                    dve.bn_stats(stats[:, t, :], z[:, t, :]).then_inc(stat_step.sem, 1)
                m = u * STAT_PER
                dve.wait_ge(stat_step.sem, stat_step.at(rnd, m + TB))
                dve.sem_inc(aggregation_begun, 1)
                for t in range(TB):
                    dve.bn_aggr(mean_var[:, t, :], stats[:, t, :]).then_inc(stat_step.sem, 1)
                dve.wait_ge(stat_step.sem, stat_step.at(rnd, m + 2 * TB))
                dve.tensor_scalar(var_eps[:], mean_var[:, :, 1], LN_EPS, None, ALU.add).then_inc(stat_step.sem, 1)

            def normalise(rnd, u):
                dve.wait_ge(rows_ready.sem, rows_ready.at(rnd, u * TB))
                if place(u - 1)[0] < L - 1:
                    dve.wait_ge(a_full.sem, a_full.at(rnd, (u + 1) * A_PER))
                dve.wait_ge(rstd_ready.sem, rstd_ready.at(rnd, u + 1))
                for t in range(TB):
                    dve.tensor_scalar(z_hat[:, t, :], z[:, t, :], mean_var[:, t, 0:1], rstd[:, t:t + 1],
                                      ALU.subtract, ALU.mult).then_inc(z_hat_ready.sem, 1)

            def add_skip(rnd, u):
                l = u // B
                for c in range(IC):
                    n = u * C_PER + 1 + c
                    dve.wait_ge(c_full.sem, c_full.at(rnd, n + 1))
                    if c == 0:
                        dve.wait_ge(d_full.sem, d_full.at(rnd, u * D_PER))
                        dve.wait_ge(u_ready.sem, u_ready.at(rnd, (u + 1) * IC))
                    dve.scalar_tensor_tensor(out=y[:, c, :], in0=act_u[u % 2][:, c, :], scalar=d_vec[:, l, c:c + 1],
                                             in1=ring_c[n % C_RING][:], op0=ALU.mult,
                                             op1=ALU.add).then_inc(c_drained.sem, 1)

            def unit(rnd, u, first, last):
                convolve(rnd, u)
                if u >= 1 or not first:
                    row_stats(rnd, u - 1)
                recur(rnd, u)
                if u == 0:
                    embed(rnd, 1)
                if u == UNITS - 1 and not last:
                    embed(rnd + 1, 0)
                if u >= 1 or not first:
                    normalise(rnd, u - 1)
                add_skip(rnd, u)

            def finish(rnd, u):
                row_stats(rnd, u)
                normalise(rnd, u)

            embed(0, 0)
            dve.wait_ge(set_up, 3)
            dve.wait_ge(tails_zero, 4)
            dve.wait_ge(columns_in, 16 * 5)
            run(dve, unit, finish)

        @block.tensor
        def _(pe):
            for ev in (a_full, c_full, d_full):
                pe.sem_inc(ev.sem, ev.start)

            def fresh_a(rnd, n):
                pe.wait_ge(a_drained.sem, a_drained.at(rnd, n - A_RING + 1))
                return ring_a[n % A_RING]

            def fresh_c(rnd, n):
                pe.wait_ge(c_drained.sem, c_drained.at(rnd, n - C_RING + 1))
                return ring_c[n % C_RING]

            def turn(rnd, u, src):
                for k in range(KC):
                    bank = fresh_a(rnd, u * A_PER + TURNED + k)
                    for t in range(TB):
                        mm = pe.transpose(bank[:, t * P:(t + 1) * P], src[:, t, k * P:(k + 1) * P], ident[:])
                    mm.then_inc(a_full.sem, 1)

            def project(rnd, u, chunks):
                l, b = place(u)
                pe.wait_ge(a_drained.sem, a_drained.at(rnd, u * A_PER))
                for c in chunks:
                    bank = fresh_a(rnd, u * A_PER + c)
                    for k in range(KC):
                        mm = pe.matmul(bank[:], w_in[:, l, k, c * P:(c + 1) * P], x_t[b][:, k, :],
                                       start=(k == 0), stop=(k == KC - 1))
                    mm.then_inc(a_full.sem, 1)

            def project_b(rnd, u):
                bank = fresh_c(rnd, u * C_PER)
                for c in range(IC):
                    pe.wait_ge(u_ready.sem, u_ready.at(rnd, u * IC + c + 1))
                    mm = pe.matmul(bank[:], w_b[:, u // B, c, :], act_u[u % 2][:, c, :],
                                   start=(c == 0), stop=(c == IC - 1))
                mm.then_inc(c_full.sem, 1)

            def project_c(rnd, u, chunks):
                pe.wait_ge(scanned.sem, scanned.at(rnd, u + 1))
                for c in chunks:
                    bank = fresh_c(rnd, u * C_PER + 1 + c)
                    pe.matmul(bank[:], w_c[:, u // B, c * P:(c + 1) * P], hs[:],
                              start=True, stop=True).then_inc(c_full.sem, 1)

            def project_out(rnd, u):
                l = place(u)[0]
                for i in range(D_PER):
                    n = u * D_PER + i
                    pe.wait_ge(d_drained.sem, d_drained.at(rnd, n - D_RING + 1))
                    for j in range(2):
                        t = 2 * i + j
                        for c in range(IC):
                            pe.wait_ge(y_ready.sem, y_ready.at(rnd, u * IC + c + 1))
                            mm = pe.matmul(ring_d[n % D_RING][:, j, :], y[:, c, t * P:(t + 1) * P],
                                           w_out[:, l, c, :], start=(c == 0), stop=(c == IC - 1))
                    mm.then_inc(d_full.sem, 1)

            def unit(rnd, u, first, last):
                if first and u % B == 0:
                    pe.wait_ge(w_in_in[u // B], 16)
                project(rnd, u, range(0, IC))
                if first and u == 1:
                    pe.wait_ge(w_out_in, 16)
                if u >= 1 or not first:
                    project_out(rnd, u - 1)
                if first and u == 0:
                    pe.wait_ge(w_b_in, 16)
                    pe.wait_ge(w_c_in, 16)
                project_b(rnd, u)
                project(rnd, u, range(IC, 2 * IC))
                project_c(rnd, u, range(0, IC // 2))
                if u == 0 or (u == UNITS - 1 and not last):
                    pe.wait_ge(emb_added.sem, emb_added.at(rnd, 2 if u == 0 else 2 * B))
                    turn(rnd, u, resid[(u + 1) % B])
                elif u < UNITS - 1:
                    pe.wait_ge(z_hat_ready.sem, z_hat_ready.at(rnd, u * TB))
                    turn(rnd, u, z_hat)
                project_c(rnd, u, range(IC // 2, IC))

            pe.wait_ge(set_up, 3)
            pe.wait_ge(emb_added.sem, emb_added.at(0, 0))
            turn(0, -1, resid[0])
            pe.wait_ge(tails_zero, 4)
            run(pe, unit, project_out)


class Steps:

    def __init__(self, sem, per_unit, apart=0):
        self.sem, self.per_unit, self.apart = sem, per_unit, apart

    @property
    def start(self):
        return 2 * self.per_unit + self.apart

    def done(self, unit, count=None):
        return self.apart + (unit + 2) * self.per_unit + (self.per_unit if count is None else count)


def build_latent(nc, d, rows_in, x_t, c_t):
    TOKENS, D = rows_in.shape
    KC = D // P
    GRP = 512
    TB = GRP // P
    GROUPS = TOKENS // GRP
    PAR, BANKS = 4, 2
    with ExitStack() as ctx:
        def sb(name, shape, dt=F32):
            return ctx.enter_context(nc.sbuf_tensor(name, shape, dt))

        def sem(name):
            return ctx.enter_context(nc.semaphore(name))

        w_down = sb("la_w_down", [P, KC, P])
        ident = sb("la_ident", [P, P])
        minus_half = sb("la_minus_half", [P, TB])
        rows = [sb(f"la_rows{i}", [P, TB, D]) for i in range(PAR)]
        z_hat = [sb(f"la_z_hat{i}", [P, TB, D]) for i in range(PAR)]
        stats = [sb(f"la_stats{i}", [P, TB, 6]) for i in range(PAR)]
        mean_var = [sb(f"la_mean_var{i}", [P, TB, 2]) for i in range(PAR)]
        var_eps = [sb(f"la_var_eps{i}", [P, TB]) for i in range(PAR)]
        rstd = [sb(f"la_rstd{i}", [P, TB]) for i in range(PAR)]
        turned = [[ctx.enter_context(nc.psum_tensor(f"la_turned{i}{k}", [P, GRP], F32)) for k in range(KC)]
                  for i in range(BANKS)]
        latent = [ctx.enter_context(nc.psum_tensor(f"la_latent{i}", [P, GRP], F32)) for i in range(BANKS)]

        w_down_in = sem("la_w_down_in")
        ident_zero = sem("la_ident_zero")
        set_up = sem("la_set_up")
        rows_in_sem = [sem(f"la_rows_in{i}") for i in range(PAR)]
        stat_step = Steps(sem("la_stat_step"), 2 * TB + 1)
        aggregation_begun = sem("la_aggregation_begun")
        rstd_ready = Steps(sem("la_rstd_ready"), 1)
        z_ready = Steps(sem("la_z_ready"), TB, PAR * TB)
        turned_full = Steps(sem("la_turned_full"), KC, PAR * KC)
        x_ready = Steps(sem("la_x_ready"), KC)
        latent_full = Steps(sem("la_latent_full"), 1)
        c_ready = Steps(sem("la_c_ready"), 1)
        block = ctx.enter_context(nc.Block())

        @block.sync
        def _(sp):
            sp.dma_start(w_down[:], d["w_kv_down"].rearrange("(k p) r -> p k r", p=P)).then_inc(w_down_in, 16)
            with sp.Fori(0, GROUPS // PAR) as rnd:
                for i in range(PAR):
                    g = rnd * PAR + i
                    sp.wait_ge(z_ready.sem, z_ready.done(g - PAR))
                    sp.dma_start(rows[i][:], rows_in[bass.ds(g * GRP, GRP), :]
                                 .rearrange("(t p) n -> p t n", p=P)).then_inc(rows_in_sem[i], 16)

        @block.gpsimd
        def _(pool):
            pool.sem_inc(rstd_ready.sem, rstd_ready.start)
            pool.memset(minus_half[:], -0.5).then_inc(ident_zero, 1)
            pool.memset(ident[:], 0.0).then_inc(ident_zero, 1)
            pool.wait_ge(ident_zero, 2)
            pool.affine_select(out=ident[:], in_=ident[:], compare_op=ALU.not_equal, fill=1.0, base=0,
                               pattern=[[-1, P]], channel_multiplier=1).then_inc(set_up, 1)
            with pool.Fori(0, GROUPS // PAR) as rnd:
                for i in range(PAR):
                    g = rnd * PAR + i
                    pool.wait_ge(stat_step.sem, stat_step.done(g))
                    pool.tensor_tensor(rstd[i][:], var_eps[i][:], minus_half[:],
                                       ALU.pow).then_inc(rstd_ready.sem, 1)

        @block.vector
        def _(dve):
            dve.sem_inc(stat_step.sem, stat_step.start)
            dve.sem_inc(z_ready.sem, z_ready.start)

            def row_stats(g, i, landed):
                dve.wait_ge(rows_in_sem[i], landed)
                for t in range(TB):
                    dve.bn_stats(stats[i][:, t, :], rows[i][:, t, :]).then_inc(stat_step.sem, 1)
                dve.wait_ge(stat_step.sem, stat_step.done(g, TB))
                dve.sem_inc(aggregation_begun, 1)
                for t in range(TB):
                    dve.bn_aggr(mean_var[i][:, t, :], stats[i][:, t, :]).then_inc(stat_step.sem, 1)
                dve.wait_ge(stat_step.sem, stat_step.done(g, 2 * TB))
                dve.tensor_scalar(var_eps[i][:], mean_var[i][:, :, 1], LN_EPS, None,
                                  ALU.add).then_inc(stat_step.sem, 1)

            def normalise(g, i):
                dve.wait_ge(rstd_ready.sem, rstd_ready.done(g))
                dve.wait_ge(turned_full.sem, turned_full.done(g - PAR))
                for t in range(TB):
                    dve.tensor_scalar(z_hat[i][:, t, :], rows[i][:, t, :], mean_var[i][:, t, 0:1],
                                      rstd[i][:, t:t + 1], ALU.subtract, ALU.mult).then_inc(z_ready.sem, 1)

            with dve.Fori(0, GROUPS // PAR) as rnd:
                for i in range(PAR):
                    row_stats(rnd * PAR + i, i, (rnd + 1) * 16)
                    if i % 2 == 1:
                        normalise(rnd * PAR + i - 1, i - 1)
                        normalise(rnd * PAR + i, i)

        @block.tensor
        def _(pe):
            pe.sem_inc(turned_full.sem, turned_full.start)
            pe.sem_inc(latent_full.sem, latent_full.start)
            pe.wait_ge(set_up, 1)
            pe.wait_ge(w_down_in, 16)
            with pe.Fori(0, GROUPS // PAR) as rnd:
                for i in range(PAR):
                    g = rnd * PAR + i
                    pe.wait_ge(z_ready.sem, z_ready.done(g))
                    pe.wait_ge(x_ready.sem, x_ready.done(g - BANKS))
                    for k in range(KC):
                        for t in range(TB):
                            mm = pe.transpose(turned[i % BANKS][k][:, t * P:(t + 1) * P],
                                              z_hat[i][:, t, k * P:(k + 1) * P], ident[:])
                        mm.then_inc(turned_full.sem, 1)
                    if i % BANKS == BANKS - 1:
                        for j in range(i + 1 - BANKS, i + 1):
                            g = rnd * PAR + j
                            pe.wait_ge(x_ready.sem, x_ready.done(g))
                            pe.wait_ge(c_ready.sem, c_ready.done(g - BANKS))
                            for k in range(KC):
                                mm = pe.matmul(latent[j % BANKS][:], w_down[:, k, :],
                                               x_t[:, k, bass.ds(g * GRP, GRP)], start=(k == 0), stop=(k == KC - 1))
                            mm.then_inc(latent_full.sem, 1)

        @block.scalar
        def _(act):
            act.sem_inc(x_ready.sem, x_ready.start)
            act.sem_inc(c_ready.sem, c_ready.start)
            with act.Fori(0, GROUPS // PAR) as rnd:
                for i in range(PAR):
                    g = rnd * PAR + i
                    for k in range(KC):
                        act.wait_ge(turned_full.sem, turned_full.done(g, k + 1))
                        act.activation(x_t[:, k, bass.ds(g * GRP, GRP)], turned[i % BANKS][k][:],
                                       ACT.Copy).then_inc(x_ready.sem, 1)
                    if i % BANKS == BANKS - 1:
                        for j in range(i + 1 - BANKS, i + 1):
                            g = rnd * PAR + j
                            act.wait_ge(latent_full.sem, latent_full.done(g))
                            act.activation(c_t[:, bass.ds(g * GRP, GRP)], latent[j % BANKS][:],
                                           ACT.Copy).then_inc(c_ready.sem, 1)


def build_attention(nc, d, x_t, c_t, o_t, sums):
    TOKENS = c_t.shape[1]
    B = 2
    T = TOKENS // B
    KC = x_t.shape[1]
    PAIRS = d["w_q"].shape[0]
    HD = P // 2
    VW = HD + 2
    SCALE = float(HD) ** -0.5
    QB = 512
    NQB, NKC, NQT = T // QB, T // P, T // P
    KPQ = QB // P
    MASKED = -1e30
    LOWEST = -3.0e38
    STEPS = [(qb, kc) for qb in range(NQB) for kc in range(KPQ * (qb + 1))]
    NS = len(STEPS)
    ENDS = [max(s for s, (q, _) in enumerate(STEPS) if q == qb) for qb in range(NQB)]
    UNITS = [(i, j) for i in range(NQT) for j in range(i // KPQ + 1)]
    NU = len(UNITS)
    HEADS_PER_ROUND = 2 * B
    JOBS = PAIRS * HEADS_PER_ROUND
    LAG = 4
    S_RING, E_RING, O_RING, MAX_RING = 2, 5, 2, 3
    assert NS % E_RING == 0 and NS % S_RING == 0 and NQB % O_RING == 0 and LAG < E_RING

    with ExitStack() as ctx:
        def sb(name, shape, dt=F32):
            return ctx.enter_context(nc.sbuf_tensor(name, shape, dt))

        def psum(name, shape):
            return ctx.enter_context(nc.psum_tensor(name, shape, F32))

        def sem(name):
            return ctx.enter_context(nc.semaphore(name))

        def steps(name, per_unit, apart=0):
            return Steps(sem(name), per_unit, apart)

        w_q = sb("at_w_q", [P, KC, P])
        w_k = sb("at_w_k", [P, P])
        w_v = sb("at_w_v", [P, P])
        q_raw = sb("at_q_raw", [P, T])
        k_raw = sb("at_k_raw", [P, T])
        v_raw = [sb(f"at_v_raw{i}", [P, KPQ, 2, HD]) for i in range(2)]
        q_hl = [sb(f"at_q_hl{h}", [P, T], F32R) for h in range(2)]
        q_hm = [sb(f"at_q_hm{h}", [P, T], F32R) for h in range(2)]
        k_hh = [sb(f"at_k_hh{h}", [P, T], F32R) for h in range(2)]
        k_lo = [sb(f"at_k_lo{h}", [P, T], F32R) for h in range(2)]
        v_hi = [sb(f"at_v_hi{b}", [P, NKC, 2, VW], F32R) for b in range(B)]
        v_lo = [sb(f"at_v_lo{b}", [P, NKC, 2, VW], F32R) for b in range(B)]
        e = [sb(f"at_e{i}", [P, QB]) for i in range(E_RING)]
        e_hi = [sb(f"at_e_hi{i}", [P, QB], F32R) for i in range(E_RING)]
        e_lo = [sb(f"at_e_lo{i}", [P, QB], F32R) for i in range(E_RING)]
        o_sb = [sb(f"at_o_sb{i}", [VW, QB]) for i in range(O_RING)]
        part_max = sb("at_part_max", [P, NQT, NQB])
        row_max = sb("at_row_max", [P, NQT])
        minus_max = sb("at_minus_max", [P, NQT, VW], F32R)
        ident_f = sb("at_ident_f", [P, P])
        ident_r = sb("at_ident_r", [P, P], F32R)
        ident_b = sb("at_ident_b", [P, P], BF16)
        mask_qk = sb("at_mask_qk", [P, P], BF16)
        mask_kq = sb("at_mask_kq", [P, P], BF16)
        ps_max = [psum(f"at_ps_max{i}", [P, QB]) for i in range(MAX_RING)]
        ps_s = [psum(f"at_ps_s{i}", [P, QB]) for i in range(S_RING)]
        ps_o = [psum(f"at_ps_o{i}", [VW, QB]) for i in range(O_RING)]
        ps_m = psum("at_ps_m", [P, QB])
        zeros = e[0]

        w_qk_in = sem("at_w_qk_in")
        w_v_in = sem("at_w_v_in")
        zeroed = sem("at_zeroed")
        masks_set = sem("at_masks_set")
        constants = sem("at_constants")
        halves_zero = sem("at_halves_zero")
        CONSTANTS = 1 + NQB + 2 * B + 2 * NQB
        NP = 2 * NQB
        proj_full = steps("at_proj_full", NP)
        proj_drained = steps("at_proj_drained", NP)
        v_full = steps("at_v_full", NQB)
        v_drained = steps("at_v_drained", NQB)
        v_rounded = steps("at_v_rounded", NQB)
        v_split = steps("at_v_split", NQB)
        turned = steps("at_turned", NQB)
        turned_drained = steps("at_turned_drained", NQB)
        k_dup = steps("at_k_dup", NQB)
        k_hi = steps("at_k_hi", NQB)
        q_hi = steps("at_q_hi", NQB)
        q_hi2 = steps("at_q_hi2", NQB)
        los = steps("at_los", 2 * NQB)
        max_full = steps("at_max_full", NU, 400)
        max_read = steps("at_max_read", NU, 200)
        max_step = steps("at_max_step", 3 * NQB)
        s_full = steps("at_s_full", NS)
        e_ready = steps("at_e_ready", NS)
        e_rounded = steps("at_e_rounded", NS)
        rounding_begun = sem("at_rounding_begun")
        e_split_dve = steps("at_e_split_dve", NS - NS // E_RING)
        e_split_pool = steps("at_e_split_pool", NS // E_RING)
        pv_done = steps("at_pv_done", NS, 600)
        o_copied = steps("at_o_copied", NQB)
        o_stored = [sem(f"at_o_stored{i}") for i in range(O_RING)]
        STORES = 32

        block = ctx.enter_context(nc.Block())

        def split_done(g, s):
            turn, slot = divmod(s, E_RING)
            if slot == E_RING - 1:
                return e_split_pool.sem, e_split_pool.done(g, turn + 1)
            return e_split_dve.sem, e_split_dve.done(g, (E_RING - 1) * turn + slot + 1)

        def projects_values(hh, rnd, runs):
            last = isinstance(rnd, int) and rnd == PAIRS - 1 and hh == HEADS_PER_ROUND - 2
            return (hh % 2 == 0 or not runs) and not last

        def weave(hh, rnd, runs, more):
            at = {s: [] for s in range(NS)}
            if not more:
                return at
            if hh % 2 == 1:
                for n in range(NP):
                    at[n + n // 2].append(("proj", n, n // 2 + n % 2 * NQB))
            first, after = 3 if hh % 2 == 1 else 1, NP + NP // 2
            for c in range(NQB):
                at[first - 1 + (3 if hh % 2 == 1 else 2) * c].append(("split", c, c))
            if projects_values(hh, rnd, runs):
                for c in range(NQB):
                    at[after + 1 + 2 * c].append(("v", c, c))
                    at[after + 2 + 2 * c].append(("v_split", c, c))
            last = NS - 2
            for n, (i, u) in enumerate(UNITS):
                s = max(first + n * (last - first) // NU, first + 3 * (i // KPQ))
                at[s].append(("max", n, (i, u)))
                if i % KPQ == KPQ - 1 and u == i // KPQ:
                    at[s].append(("max_end", u, u))
                    at[max(s + 2, after + 2 * NQB + 1 + u)].append(("turn", u, u))
            return at

        def ahead(s, n):
            return divmod(s + n, NS)

        def run(eng, job, counted):
            for ev in counted:
                eng.sem_inc(ev.sem, ev.start)
            job(-1, HEADS_PER_ROUND - 1, -1, True, False)
            with eng.Fori(0, PAIRS - 1) as rnd:
                for hh in range(HEADS_PER_ROUND):
                    job(rnd * HEADS_PER_ROUND + hh, hh, rnd, True, True)
            for hh in range(HEADS_PER_ROUND):
                more = hh < HEADS_PER_ROUND - 1
                job((PAIRS - 1) * HEADS_PER_ROUND + hh, hh, PAIRS - 1, more, True)

        @block.sync
        def _(sp):
            def load_qk(pair):
                one = bass.ds(pair, 1)
                sp.dma_start(w_q[:], d["w_q"][one].rearrange("a p k n -> (a p) k n")).then_inc(w_qk_in, 16)
                sp.dma_start(w_k[:], d["w_k"][one].rearrange("a p n -> (a p) n")).then_inc(w_qk_in, 16)

            def load_v(pair):
                sp.dma_start(w_v[:], d["w_v"][bass.ds(pair, 1)].rearrange("a p n -> (a p) n")).then_inc(w_v_in, 16)

            def store(g, hh, rnd):
                b, h = hh // 2, hh % 2
                for qb in range(NQB):
                    cols = slice(b * T + qb * QB, b * T + (qb + 1) * QB)
                    i = qb % O_RING
                    sp.wait_ge(o_copied.sem, o_copied.done(g, qb + 1))
                    sp.dma_start(o_t[bass.ds(rnd * P + h * HD, HD), cols], o_sb[i][0:HD, :]).then_inc(o_stored[i], 16)
                    sp.dma_start(sums[bass.ds(rnd * 2 + h, 1), cols], o_sb[i][HD:HD + 1, :]).then_inc(o_stored[i], 16)

            for i in range(O_RING):
                sp.sem_inc(o_stored[i], STORES)
            load_qk(0)
            load_v(0)
            with sp.Fori(0, PAIRS - 1) as rnd:
                for hh in range(HEADS_PER_ROUND):
                    if hh == 1:
                        sp.wait_ge(v_full.sem, v_full.done(rnd * B + 1))
                        load_v(rnd + 1)
                    if hh == 2:
                        sp.wait_ge(proj_full.sem, proj_full.done(rnd * B + 1))
                        load_qk(rnd + 1)
                    store(rnd * HEADS_PER_ROUND + hh, hh, rnd)
            for hh in range(HEADS_PER_ROUND):
                store((PAIRS - 1) * HEADS_PER_ROUND + hh, hh, PAIRS - 1)
            for i in range(O_RING):
                sp.wait_ge(o_stored[i], STORES * (1 + JOBS * NQB // O_RING))

        @block.gpsimd
        def _(pool):
            pool.memset(ident_f[:], 0.0).then_inc(zeroed, 1)
            pool.memset(ident_b[:], 0.0).then_inc(zeroed, 1)
            pool.memset(mask_qk[:], 0.0).then_inc(zeroed, 1)
            pool.memset(mask_kq[:], 0.0).then_inc(zeroed, 1)
            pool.memset(zeros[:], 0.0).then_inc(zeroed, 1)
            pool.wait_ge(zeroed, 5)
            for m in (ident_f, ident_b):
                pool.affine_select(out=m[:], in_=m[:], compare_op=ALU.not_equal, fill=1.0, base=0,
                                   pattern=[[-1, P]], channel_multiplier=1).then_inc(masks_set, 1)
            pool.affine_select(out=mask_qk[:], in_=mask_qk[:], compare_op=ALU.is_ge, fill=MASKED, base=0,
                               pattern=[[-1, P]], channel_multiplier=1).then_inc(masks_set, 1)
            pool.affine_select(out=mask_kq[:], in_=mask_kq[:], compare_op=ALU.is_ge, fill=MASKED, base=0,
                               pattern=[[1, P]], channel_multiplier=-1).then_inc(masks_set, 1)
            pool.memset(part_max[:], LOWEST).then_inc(masks_set, 1)

            def job(g, hh, rnd, more, runs):
                h = (hh + 1) % 2
                j, jv = rnd * B + (hh + 1) // 2, rnd * B + hh // 2 + 1
                bv = (hh // 2 + 1) % B
                hi = slice(h * HD, h * HD + HD)
                todo = weave(hh, rnd, runs, more)
                for s in range(NS):
                    on, sn = ahead(s, LAG - 1)
                    if (more if on else runs) and sn % E_RING == E_RING - 1:
                        qb, kc = STEPS[sn]
                        off = max(0, kc - KPQ * qb) * P
                        pool.wait_ge(e_rounded.sem, e_rounded.done(g + on, sn + 1))
                        pool.sem_inc(rounding_begun, 1)
                        pool.tensor_tensor(e_lo[sn % E_RING][:, off:], e[sn % E_RING][:, off:],
                                           e_hi[sn % E_RING][:, off:].bitcast(F32),
                                           ALU.subtract).then_inc(e_split_pool.sem, 1)
                    on, sn = ahead(s, LAG)
                    if (more if on else runs):
                        qb, kc = STEPS[sn]
                        off = max(0, kc - KPQ * qb) * P
                        pool.wait_ge(e_ready.sem, e_ready.done(g + on, sn + 1))
                        pool.wait_ge(pv_done.sem, pv_done.done(g + on, sn + 1 - E_RING))
                        pool.sem_inc(rounding_begun, 1)
                        pool.tensor_scalar(e_hi[sn % E_RING][:, off:], e[sn % E_RING][:, off:], 1.0, 1.0, ALU.mult,
                                           ALU.mult).then_inc(e_rounded.sem, 1)
                    for what, n, c in todo[s]:
                        if what == "split":
                            cs = slice(c * QB, (c + 1) * QB)
                            on, sn = ahead(s, LAG)
                            pool.wait_ge(e_rounded.sem, e_rounded.done(g + on, sn + 1))
                            on, sn = ahead(s, LAG - 1)
                            pool.wait_ge(e_split_pool.sem, e_split_pool.done(g + on, (sn + 1) // E_RING))
                            pool.wait_ge(q_hi.sem, q_hi.done(g + 1, c + 1))
                            pool.sem_inc(rounding_begun, 1)
                            pool.tensor_scalar(q_hm[h][hi, cs], q_hl[h][hi, cs].bitcast(F32), 1.0, 1.0, ALU.mult,
                                               ALU.mult).then_inc(q_hi2.sem, 1)
                            pool.wait_ge(q_hi2.sem, q_hi2.done(g + 1, c + 1))
                            pool.sem_inc(rounding_begun, 1)
                        elif what == "v_split":
                            pool.wait_ge(v_drained.sem, v_drained.done(jv, c + 1))
                            pool.wait_ge(pv_done.sem, pv_done.done(g - 1))
                            pool.sem_inc(rounding_begun, 1)
                            pool.tensor_scalar(v_hi[bv][:, c * KPQ:(c + 1) * KPQ, :, 0:HD], v_raw[c % 2][:], 1.0, 1.0,
                                               ALU.mult, ALU.mult).then_inc(v_rounded.sem, 1)

            run(pool, job, [q_hi2, e_rounded, e_split_pool, v_rounded])

        @block.scalar
        def _(act):
            act.wait_ge(masks_set, 5)
            act.wait_ge(zeroed, 5)
            act.activation(ident_r[:], ident_f[:], ACT.Copy).then_inc(constants, 1)
            for i in range(NQB):
                act.activation(minus_max[:, i * KPQ:(i + 1) * KPQ, :],
                               zeros[:, 0:KPQ * VW].rearrange("p (a b) -> p a b", a=KPQ),
                               ACT.Copy).then_inc(constants, 1)
            for b in range(B):
                for v, ones in ((v_hi, 1.0), (v_lo, 0.0)):
                    act.activation(v[b][:, :, :, HD:], zeros[:, 0:NKC * 4].rearrange("p (a b c) -> p a b c", a=NKC, b=2),
                                   ACT.Copy, bias=ones).then_inc(constants, 1)
            act.wait_ge(halves_zero, 4 * NQB)
            for h in range(2):
                row = (1 - h) * HD
                for c in range(NQB):
                    cs = slice(c * QB, (c + 1) * QB)
                    act.activation(k_lo[h][row:row + 1, cs], zeros[row:row + 1, :], ACT.Copy,
                                   bias=1.0).then_inc(constants, 1)
            act.wait_ge(constants, CONSTANTS)

            def job(g, hh, rnd, more, runs):
                hn = (hh + 1) % 2
                hi = slice(hn * HD, hn * HD + HD)
                other = slice((1 - hn) * HD, (1 - hn) * HD + HD)
                j, jv = rnd * B + (hh + 1) // 2, rnd * B + hh // 2 + 1
                bv = (hh // 2 + 1) % B
                row = (1 - hn) * HD
                todo = weave(hh, rnd, runs, more)
                for s in range(NS):
                    for what, n, c in todo[s]:
                        if what == "proj":
                            act.wait_ge(proj_full.sem, proj_full.done(j, n + 1))
                            cs = slice((c % NQB) * QB, (c % NQB + 1) * QB)
                            if c < NQB:
                                if c == 0:
                                    act.wait_ge(los.sem, los.done(g))
                                act.activation(q_raw[:, cs], ps_m[:], ACT.Copy).then_inc(proj_drained.sem, 1)
                            else:
                                act.activation(k_raw[:, cs], ps_m[:], ACT.Copy).then_inc(proj_drained.sem, 1)
                        elif what == "v":
                            act.wait_ge(v_split.sem, v_split.done(jv, c - 1))
                            act.wait_ge(v_full.sem, v_full.done(jv, c + 1))
                            act.activation(v_raw[c % 2][:], ps_m[:].rearrange("p (t h n) -> p t h n", t=KPQ, h=2),
                                           ACT.Copy).then_inc(v_drained.sem, 1)
                        elif what == "split":
                            cs = slice(c * QB, (c + 1) * QB)
                            act.wait_ge(pv_done.sem, pv_done.done(g - 1))
                            act.wait_ge(proj_drained.sem, proj_drained.done(j, 2 * (c + 1)))
                            act.activation(q_hl[hn][hi, cs], q_raw[hi, cs], ACT.Copy).then_inc(q_hi.sem, 1)
                            act.activation(k_hh[hn][hi, cs], k_raw[hi, cs], ACT.Copy).then_inc(k_hi.sem, 1)
                            act.activation(k_hh[hn][other, cs], k_raw[hi, cs], ACT.Copy).then_inc(k_dup.sem, 1)
                        elif what == "turn":
                            cs = slice(c * QB, (c + 1) * QB)
                            act.wait_ge(turned.sem, turned.done(g + 1, c + 1))
                            act.activation(q_hm[hn][row:row + 1, cs], ps_m[row:row + 1, :],
                                           ACT.Copy).then_inc(turned_drained.sem, 1)
                    on, sn = ahead(s, LAG)
                    if (more if on else runs):
                        qb, kc = STEPS[sn]
                        off = max(0, kc - KPQ * qb) * P
                        act.wait_ge(s_full.sem, s_full.done(g + on, sn + 1))
                        act.wait_ge(*split_done(g + on, sn - E_RING))
                        act.activation(e[sn % E_RING][:, off:], ps_s[sn % S_RING][:, off:], ACT.Exp,
                                       scale=SCALE).then_inc(e_ready.sem, 1)
                    if runs and s in ENDS:
                        qb = ENDS.index(s)
                        act.wait_ge(pv_done.sem, pv_done.done(g, s + 1))
                        act.wait_ge(o_stored[qb % O_RING], (g * (NQB // O_RING) + qb // O_RING + 1) * STORES)
                        act.activation(o_sb[qb % O_RING][:], ps_o[qb % O_RING][:], ACT.Copy).then_inc(o_copied.sem, 1)

            run(act, job, [proj_drained, v_drained, turned_drained, q_hi, k_hi, k_dup, e_ready, o_copied])

        @block.vector
        def _(dve):
            dve.wait_ge(zeroed, 5)
            for h in range(2):
                other = slice((1 - h) * HD, (1 - h) * HD + HD)
                for c in range(NQB):
                    cs = slice(c * QB, (c + 1) * QB)
                    dve.tensor_copy(q_hm[h][other, cs], zeros[other, :]).then_inc(halves_zero, 1)
                    dve.tensor_copy(k_lo[h][other, cs], zeros[other, :]).then_inc(halves_zero, 1)

            def job(g, hh, rnd, more, runs):
                hn = (hh + 1) % 2
                hi = slice(hn * HD, hn * HD + HD)
                other = slice((1 - hn) * HD, (1 - hn) * HD + HD)
                j, jv = rnd * B + (hh + 1) // 2, rnd * B + hh // 2 + 1
                bv = (hh // 2 + 1) % B
                todo = weave(hh, rnd, runs, more)
                for s in range(NS):
                    for what, n, c in todo[s]:
                        if what == "split":
                            cs = slice(c * QB, (c + 1) * QB)
                            dve.wait_ge(pv_done.sem, pv_done.done(g - 1))
                            dve.wait_ge(q_hi.sem, q_hi.done(g + 1, c + 1))
                            dve.tensor_tensor(q_hl[hn][other, cs], q_raw[hi, cs], q_hl[hn][hi, cs].bitcast(F32),
                                              ALU.subtract).then_inc(los.sem, 1)
                            dve.wait_ge(k_hi.sem, k_hi.done(g + 1, c + 1))
                            dve.tensor_tensor(k_lo[hn][hi, cs], k_raw[hi, cs], k_hh[hn][hi, cs].bitcast(F32),
                                              ALU.subtract).then_inc(los.sem, 1)
                        elif what == "v_split":
                            ts = slice(c * KPQ, (c + 1) * KPQ)
                            dve.wait_ge(v_rounded.sem, v_rounded.done(jv, c + 1))
                            dve.tensor_tensor(v_lo[bv][:, ts, :, 0:HD], v_raw[c % 2][:],
                                              v_hi[bv][:, ts, :, 0:HD].bitcast(F32),
                                              ALU.subtract).then_inc(v_split.sem, 1)
                        elif what == "max":
                            i, u = c
                            w = min((i + 1) * P - u * QB, QB)
                            dve.wait_ge(max_full.sem, max_full.done(g + 1, n + 1))
                            dve.tensor_reduce(part_max[:, i, u:u + 1], ps_max[n % MAX_RING][:, 0:w], AX.X,
                                              ALU.max).then_inc(max_read.sem, 1)
                        elif what == "max_end":
                            ts = slice(c * KPQ, (c + 1) * KPQ)
                            so_far = sum(1 for i, _ in UNITS if i < (c + 1) * KPQ)
                            dve.wait_ge(max_read.sem, max_read.done(g + 1, so_far))
                            dve.tensor_reduce(row_max[:, ts], part_max[:, ts, :], AX.X,
                                              ALU.max).then_inc(max_step.sem, 1)
                            dve.wait_ge(max_step.sem, max_step.done(g + 1, 3 * c + 1))
                            dve.wait_ge(turned.sem, turned.done(g, c + 1))
                            for col in (0, HD):
                                dve.tensor_scalar(minus_max[:, ts, col], row_max[:, ts], -1.0, None,
                                                  ALU.mult).then_inc(max_step.sem, 1)
                    on, sn = ahead(s, LAG - 1)
                    if (more if on else runs) and sn % E_RING < E_RING - 1:
                        qb, kc = STEPS[sn]
                        off = max(0, kc - KPQ * qb) * P
                        dve.wait_ge(e_rounded.sem, e_rounded.done(g + on, sn + 1))
                        dve.tensor_tensor(e_lo[sn % E_RING][:, off:], e[sn % E_RING][:, off:],
                                          e_hi[sn % E_RING][:, off:].bitcast(F32),
                                          ALU.subtract).then_inc(e_split_dve.sem, 1)

            run(dve, job, [los, max_read, max_step, e_split_dve, v_split])

        @block.tensor
        def _(pe):
            def scores(g, s, h):
                qb, kc = STEPS[s]
                off = max(0, kc - KPQ * qb) * P
                keys, queries = slice(kc * P, (kc + 1) * P), slice(qb * QB + off, (qb + 1) * QB)
                if kc == 0:
                    pe.wait_ge(turned_drained.sem, turned_drained.done(g, qb + 1))
                    pe.wait_ge(q_hi2.sem, q_hi2.done(g, qb + 1))
                pe.wait_ge(e_ready.sem, e_ready.done(g, s + 1 - S_RING))
                out = ps_s[s % S_RING]
                pe.matmul(out[:, off:], k_hh[h][:, keys], q_hl[h][:, queries], start=True, stop=False)
                diagonal = kc >= KPQ * qb
                mm = pe.matmul(out[:, off:], k_lo[h][:, keys], q_hm[h][:, queries], start=False, stop=not diagonal)
                if diagonal:
                    mm = pe.matmul(out[:, off:off + P], ident_b[:], mask_kq[:], start=False, stop=True)
                mm.then_inc(s_full.sem, 1)

            def values(g, s, h, b):
                qb, kc = STEPS[s]
                off = max(0, kc - KPQ * qb) * P
                out, i = ps_o[qb % O_RING], s % E_RING
                if kc == 0:
                    pe.wait_ge(o_copied.sem, o_copied.done(g, qb + 1 - O_RING))
                pe.wait_ge(*split_done(g, s))
                pe.matmul(out[:, off:], v_hi[b][:, kc, h, :], e_hi[i][:, off:], start=(kc == 0), stop=False)
                pe.matmul(out[:, off:], v_hi[b][:, kc, h, :], e_lo[i][:, off:], start=False, stop=False)
                pe.matmul(out[:, off:], v_lo[b][:, kc, h, :], e_hi[i][:, off:], start=False,
                          stop=(s in ENDS)).then_inc(pv_done.sem, 1)

            def job(g, hh, rnd, more, runs):
                h, b = hh % 2, hh // 2
                hn, bn = (hh + 1) % 2, ((hh + 1) // 2) % B
                j, jv = rnd * B + (hh + 1) // 2, rnd * B + hh // 2 + 1
                bv = (hh // 2 + 1) % B
                todo = weave(hh, rnd, runs, more)
                if runs and hn == 1:
                    pe.wait_ge(v_split.sem, v_split.done(rnd * B + b))
                for s in range(NS):
                    for what, n, c in todo[s]:
                        if what == "proj":
                            at = bn * T + (c % NQB) * QB
                            if n == 0:
                                pe.wait_ge(turned_drained.sem, turned_drained.done(g))
                                pe.wait_ge(w_qk_in, weights_in(rnd, hh, 32))
                            pe.wait_ge(proj_drained.sem, proj_drained.done(j, n))
                            if c < NQB:
                                for k in range(KC):
                                    mm = pe.matmul(ps_m[:], w_q[:, k, :], x_t[:, k, at:at + QB], start=(k == 0),
                                                   stop=(k == KC - 1))
                            else:
                                mm = pe.matmul(ps_m[:], w_k[:], c_t[:, at:at + QB], start=True, stop=True)
                            mm.then_inc(proj_full.sem, 1)
                        elif what == "v":
                            at = bv * T + c * QB
                            if c == 0:
                                pe.wait_ge(w_v_in, weights_in(rnd, hh, 16))
                                pe.wait_ge(turned_drained.sem, turned_drained.done(g))
                                pe.wait_ge(proj_drained.sem, proj_drained.done(j))
                            pe.wait_ge(v_drained.sem, v_drained.done(jv, c))
                            for t in range(KPQ):
                                mm = pe.matmul(ps_m[:, t * P:(t + 1) * P], c_t[:, at + t * P:at + (t + 1) * P],
                                               w_v[:], start=True, stop=True)
                            mm.then_inc(v_full.sem, 1)
                        elif what == "max":
                            i, u = c
                            if n == 0 and not runs:
                                pe.wait_ge(masks_set, 5)
                                pe.wait_ge(constants, CONSTANTS)
                            if u == 0 and i % KPQ == 0:
                                pe.wait_ge(los.sem, los.done(g + 1, 2 * (i // KPQ + 1)))
                                pe.wait_ge(k_dup.sem, k_dup.done(g + 1, i // KPQ + 1))
                            pe.wait_ge(max_read.sem, max_read.done(g + 1, n + 1 - MAX_RING))
                            w = min((i + 1) * P - u * QB, QB)
                            diagonal = u == i // KPQ
                            out = ps_max[n % MAX_RING]
                            mm = pe.matmul(out[:, 0:w], q_hl[hn][:, i * P:(i + 1) * P],
                                           k_hh[hn][:, u * QB:u * QB + w], start=True, stop=not diagonal)
                            if diagonal:
                                mm = pe.matmul(out[:, w - P:w], ident_b[:], mask_qk[:], start=False, stop=True)
                            mm.then_inc(max_full.sem, 1)
                        elif what == "turn":
                            if c == 0:
                                pe.wait_ge(proj_drained.sem, proj_drained.done(j))
                                if projects_values(hh, rnd, runs):
                                    pe.wait_ge(v_drained.sem, v_drained.done(jv))
                            pe.wait_ge(turned_drained.sem, turned_drained.done(g + 1, c))
                            pe.wait_ge(max_step.sem, max_step.done(g + 1, 3 * (c + 1)))
                            for t in range(KPQ):
                                mm = pe.matmul(ps_m[0:VW, t * P:(t + 1) * P], minus_max[:, c * KPQ + t, :],
                                               ident_r[:], start=True, stop=True)
                            mm.then_inc(turned.sem, 1)
                    on, sn = ahead(s, LAG)
                    if (more if on else runs):
                        scores(g + on, sn, hn if on else h)
                    if runs:
                        values(g, s, h, b)

            def weights_in(rnd, hh, per_round):
                return (rnd + 1 + (hh >= HEADS_PER_ROUND // 2)) * per_round

            run(pe, job, [proj_full, v_full, turned, max_full, s_full, pv_done])


def build_router(nc, d, o_t, sums, h_in, h_rows, x_rows, probs):
    FEAT, TOKENS = o_t.shape
    D = h_in.shape[1]
    KC, FC = D // P, FEAT // P
    E = d["w_r"].shape[2]
    HEADS = sums.shape[0]
    HALF = P // (FEAT // HEADS)
    LO = 32
    GRP = 512
    TB = GRP // P
    PAR = 2
    GROUPS = TOKENS // GRP
    ROUNDS = (GROUPS - 2) // PAR
    LANDED, STORED = 48, 32
    with ExitStack() as ctx:
        def sb(name, shape, dt=F32):
            return ctx.enter_context(nc.sbuf_tensor(name, shape, dt))

        def psum(name, shape):
            return ctx.enter_context(nc.psum_tensor(name, shape, F32))

        def sem(name):
            return ctx.enter_context(nc.semaphore(name))

        w_out = sb("ro_w_out", [P, FC, D])
        w_r = sb("ro_w_r", [P, KC, E])
        b_r = sb("ro_b_r", [P, E])
        ident = sb("ro_ident", [P, P])
        minus_half = sb("ro_minus_half", [P, TB])
        o_slab = [sb(f"ro_o_slab{i}", [P, FC, GRP]) for i in range(PAR)]
        o_scaled = [sb(f"ro_o_scaled{i}", [P, FC, GRP]) for i in range(PAR)]
        sum_rows = [sb(f"ro_sum_rows{i}", [HEADS, GRP]) for i in range(PAR)]
        inv = [sb(f"ro_inv{i}", [HEADS, GRP]) for i in range(PAR)]
        inv_r = [sb(f"ro_inv_r{i}", [P, GRP], F32R) for i in range(PAR)]
        zeros = sb("ro_zeros", [P, GRP])
        spread_f = sb("ro_spread_f", [P, FC, HALF, P // HALF])
        spread = sb("ro_spread", [P, FC, P], F32R)
        rows = [sb(f"ro_rows{i}", [P, TB, D]) for i in range(PAR)]
        h_new = [sb(f"ro_h_new{i}", [P, TB, D]) for i in range(PAR)]
        z_hat = [sb(f"ro_z_hat{i}", [P, TB, D]) for i in range(PAR)]
        z_t = [sb(f"ro_z_t{i}", [P, KC, GRP]) for i in range(PAR)]
        stats = [sb(f"ro_stats{i}", [P, TB, 6]) for i in range(PAR)]
        mean_var = [sb(f"ro_mean_var{i}", [P, TB, 2]) for i in range(PAR)]
        var_eps = [sb(f"ro_var_eps{i}", [P, TB]) for i in range(PAR)]
        rstd = [sb(f"ro_rstd{i}", [P, TB]) for i in range(PAR)]
        logits = [sb(f"ro_logits{i}", [P, TB, E]) for i in range(PAR)]
        exps = [sb(f"ro_exps{i}", [P, TB, E]) for i in range(PAR)]
        top = [sb(f"ro_top{i}", [P, TB]) for i in range(PAR)]
        total = [sb(f"ro_total{i}", [P, TB]) for i in range(PAR)]
        ps_y = [[psum(f"ro_ps_y{i}{j}", [P, 2, D]) for j in range(TB // 2)] for i in range(PAR)]
        ps_z = [psum(f"ro_ps_z{k}", [P, GRP]) for k in range(KC)]
        ps_l = psum("ro_ps_l", [P, TB, E])
        ps_inv = psum("ro_ps_inv", [P, GRP])

        consts_in = sem("ro_consts_in")
        zeroed = sem("ro_zeroed")
        set_up = sem("ro_set_up")
        loaded = [sem(f"ro_loaded{i}") for i in range(PAR)]
        stored = [sem(f"ro_stored{i}") for i in range(PAR)]
        aggregation_begun = sem("ro_aggregation_begun")
        constants = sem("ro_constants")
        inverted = Steps(sem("ro_inverted"), 1)
        inv_hi = Steps(sem("ro_inv_hi"), 1)
        inv_lo = Steps(sem("ro_inv_lo"), 1)
        inv_spread = Steps(sem("ro_inv_spread"), FC)
        scaled = Steps(sem("ro_scaled"), FC)
        y_full = Steps(sem("ro_y_full"), TB // 2)
        h_ready = Steps(sem("ro_h_ready"), TB // 2)
        stat_step = Steps(sem("ro_stat_step"), 2 * TB + 1)
        rstd_ready = Steps(sem("ro_rstd_ready"), 1)
        z_ready = Steps(sem("ro_z_ready"), TB)
        z_turned = Steps(sem("ro_z_turned"), KC)
        z_t_ready = Steps(sem("ro_z_t_ready"), KC)
        logits_full = Steps(sem("ro_logits_full"), 1)
        soft_step = Steps(sem("ro_soft_step"), 6)
        exps_ready = Steps(sem("ro_exps_ready"), 1)
        block = ctx.enter_context(nc.Block())

        def run(eng, turn):
            turn(-1, 1, -1, False, True, False)
            turn(0, 0, 0, True, True, False)
            with eng.Fori(0, ROUNDS) as rnd:
                turn(rnd * PAR + 1, 1, rnd, True, True, True)
                turn(rnd * PAR + 2, 0, rnd + 1, True, True, True)
            turn(GROUPS - 1, 1, GROUPS // PAR - 1, True, False, True)
            turn(GROUPS, 0, GROUPS // PAR, False, False, True)

        @block.sync
        def _(sp):
            for s in stored:
                sp.sem_inc(s, STORED)
            sp.dma_start(w_out[:], d["w_o"].rearrange("(c p) n -> p c n", p=P)).then_inc(consts_in, 16)
            sp.dma_start(w_r[:], d["w_r"]).then_inc(consts_in, 16)
            sp.dma_start(b_r[:], d["b_r"].partition_broadcast(P)).then_inc(consts_in, 16)
            with sp.Fori(0, GROUPS // PAR) as rnd:
                for i in range(PAR):
                    g = rnd * PAR + i
                    sp.wait_ge(scaled.sem, scaled.done(g - PAR))
                    sp.dma_start(sum_rows[i][:], sums[:, bass.ds(g * GRP, GRP)]).then_inc(loaded[i], 16)
                    sp.dma_start(o_slab[i][:], o_t.rearrange("(c p) t -> p c t", p=P)
                                 [:, :, bass.ds(g * GRP, GRP)]).then_inc(loaded[i], 16)
                    sp.wait_ge(h_ready.sem, h_ready.done(g - PAR))
                    sp.dma_start(rows[i][:], h_in[bass.ds(g * GRP, GRP), :]
                                 .rearrange("(t p) n -> p t n", p=P)).then_inc(loaded[i], 16)
            for i in range(PAR):
                sp.wait_ge(stored[i], STORED * (GROUPS // PAR + 1))

        @block.gpsimd
        def _(pool):
            pool.sem_inc(rstd_ready.sem, rstd_ready.start)
            pool.memset(minus_half[:], -0.5).then_inc(zeroed, 1)
            pool.memset(ident[:], 0.0).then_inc(zeroed, 1)
            pool.memset(zeros[:], 0.0).then_inc(zeroed, 1)
            pool.memset(spread_f[:], 0.0).then_inc(zeroed, 1)
            pool.wait_ge(zeroed, 4)
            pool.affine_select(out=ident[:], in_=ident[:], compare_op=ALU.not_equal, fill=1.0, base=0,
                               pattern=[[-1, P]], channel_multiplier=1).then_inc(set_up, 1)
            for n, first in enumerate((0, LO)):
                pool.wait_ge(set_up, 1 + n)
                pool.affine_select(out=spread_f[:], in_=spread_f[:], compare_op=ALU.not_equal, fill=1.0, base=-first,
                                   pattern=[[-HALF, FC], [-1, HALF], [0, P // HALF]],
                                   channel_multiplier=1).then_inc(set_up, 1)
            with pool.Fori(0, GROUPS // PAR) as rnd:
                for i in range(PAR):
                    pool.wait_ge(stat_step.sem, stat_step.done(rnd * PAR + i))
                    pool.tensor_tensor(rstd[i][:], var_eps[i][:], minus_half[:],
                                       ALU.pow).then_inc(rstd_ready.sem, 1)

        @block.vector
        def _(dve):
            for ev in (h_ready, stat_step, z_ready, soft_step, inverted, inv_lo, scaled):
                dve.sem_inc(ev.sem, ev.start)

            def invert(i, landed):
                dve.wait_ge(loaded[i], landed)
                dve.reciprocal(inv[i][:], sum_rows[i][:]).then_inc(inverted.sem, 1)

            def split(g, i):
                dve.wait_ge(inv_hi.sem, inv_hi.done(g))
                dve.tensor_tensor(inv_r[i][LO:LO + HEADS, :], inv[i][:], inv_r[i][0:HEADS, :].bitcast(F32),
                                  ALU.subtract).then_inc(inv_lo.sem, 1)

            def scale(g, i, chunks):
                dve.wait_ge(y_full.sem, y_full.done(g - PAR))
                for c in chunks:
                    dve.wait_ge(inv_spread.sem, inv_spread.done(g, c + 1))
                    dve.tensor_tensor(o_scaled[i][:, c, :], o_slab[i][:, c, :], ps_inv[:],
                                      ALU.mult).then_inc(scaled.sem, 1)

            def add(g, i, k, j):
                if j == 0:
                    dve.wait_ge(stored[i], (k + 1) * STORED)
                dve.wait_ge(y_full.sem, y_full.done(g, j + 1))
                dve.tensor_tensor(h_new[i][:, 2 * j:2 * j + 2, :], ps_y[i][j][:], rows[i][:, 2 * j:2 * j + 2, :],
                                  ALU.add).then_inc(h_ready.sem, 1)

            def row_stats(g, i):
                dve.wait_ge(h_ready.sem, h_ready.done(g))
                for t in range(TB):
                    dve.bn_stats(stats[i][:, t, :], h_new[i][:, t, :]).then_inc(stat_step.sem, 1)
                dve.wait_ge(stat_step.sem, stat_step.done(g, TB))
                dve.sem_inc(aggregation_begun, 1)
                for t in range(TB):
                    dve.bn_aggr(mean_var[i][:, t, :], stats[i][:, t, :]).then_inc(stat_step.sem, 1)
                dve.wait_ge(stat_step.sem, stat_step.done(g, 2 * TB))
                dve.tensor_scalar(var_eps[i][:], mean_var[i][:, :, 1], LN_EPS, None,
                                  ALU.add).then_inc(stat_step.sem, 1)

            def normalise(g, i):
                dve.wait_ge(rstd_ready.sem, rstd_ready.done(g))
                dve.wait_ge(z_turned.sem, z_turned.done(g - PAR))
                for t in range(TB):
                    dve.tensor_scalar(z_hat[i][:, t, :], h_new[i][:, t, :], mean_var[i][:, t, 0:1],
                                      rstd[i][:, t:t + 1], ALU.subtract, ALU.mult).then_inc(z_ready.sem, 1)

            def softmax(g, i):
                wide = [P, TB, E]
                dve.wait_ge(logits_full.sem, logits_full.done(g))
                dve.tensor_tensor(logits[i][:], ps_l[:], b_r[:].unsqueeze(1).broadcast_to(wide),
                                  ALU.add).then_inc(soft_step.sem, 1)
                dve.wait_ge(soft_step.sem, soft_step.done(g, 1))
                dve.tensor_reduce(top[i][:], logits[i][:], AX.X, ALU.max).then_inc(soft_step.sem, 1)
                dve.wait_ge(soft_step.sem, soft_step.done(g, 2))
                dve.tensor_tensor(logits[i][:], logits[i][:], top[i][:].unsqueeze(2).broadcast_to(wide),
                                  ALU.subtract).then_inc(soft_step.sem, 1)
                dve.wait_ge(exps_ready.sem, exps_ready.done(g))
                dve.tensor_reduce(total[i][:], exps[i][:], AX.X, ALU.add).then_inc(soft_step.sem, 1)
                dve.wait_ge(soft_step.sem, soft_step.done(g, 4))
                dve.reciprocal(total[i][:], total[i][:]).then_inc(soft_step.sem, 1)
                dve.wait_ge(soft_step.sem, soft_step.done(g, 5))
                dve.tensor_tensor(probs[:, bass.ds(g * TB, TB), :], exps[i][:],
                                  total[i][:].unsqueeze(2).broadcast_to(wide), ALU.mult).then_inc(soft_step.sem, 1)

            def turn(g, i, k, now, after, before):
                if after:
                    invert(1 - i, (k + 1 + i) * LANDED)
                    split(g + 1, 1 - i)
                if now:
                    add(g, i, k, 0)
                if before:
                    softmax(g - 1, 1 - i)
                if after:
                    scale(g + 1, 1 - i, range(FC))
                if now:
                    add(g, i, k, 1)
                    row_stats(g, i)
                    normalise(g, i)

            run(dve, turn)

        @block.tensor
        def _(pe):
            for ev in (y_full, z_turned, logits_full, inv_spread):
                pe.sem_inc(ev.sem, ev.start)
            pe.wait_ge(set_up, 3)
            pe.wait_ge(constants, 2 + PAR)
            pe.wait_ge(consts_in, 48)
            def spread_inverse(g, i, c):
                if c == 0:
                    pe.wait_ge(inv_lo.sem, inv_lo.done(g))
                pe.wait_ge(scaled.sem, scaled.done(g, c))
                pe.matmul(ps_inv[:], spread[:, c, :], inv_r[i][:], start=True, stop=True).then_inc(inv_spread.sem, 1)

            def product(g, i, t, between=None):
                if t == 0:
                    pe.wait_ge(scaled.sem, scaled.done(g))
                    pe.wait_ge(h_ready.sem, h_ready.done(g - PAR))
                for c in range(FC):
                    if between and c % 2 == 0:
                        between(c // 2)
                    mm = pe.matmul(ps_y[i][t // 2][:, t % 2, :], o_scaled[i][:, c, t * P:(t + 1) * P],
                                   w_out[:, c, :], start=(c == 0), stop=(c == FC - 1))
                if t % 2:
                    mm.then_inc(y_full.sem, 1)

            def turn_rows(g, i):
                pe.wait_ge(z_ready.sem, z_ready.done(g))
                pe.wait_ge(z_t_ready.sem, z_t_ready.done(g - 1))
                for k in range(KC):
                    for t in range(TB):
                        mm = pe.transpose(ps_z[k][:, t * P:(t + 1) * P], z_hat[i][:, t, k * P:(k + 1) * P], ident[:])
                    mm.then_inc(z_turned.sem, 1)

            def route(g, i):
                pe.wait_ge(z_t_ready.sem, z_t_ready.done(g))
                pe.wait_ge(soft_step.sem, soft_step.done(g - 1, 1))
                for t in range(TB):
                    for k in range(KC):
                        mm = pe.matmul(ps_l[:, t, :], z_t[i][:, k, t * P:(t + 1) * P], w_r[:, k, :],
                                       start=(k == 0), stop=(k == KC - 1))
                mm.then_inc(logits_full.sem, 1)

            def turn(g, i, k, now, after, before):
                if now:
                    product(g, i, 0)
                if before:
                    turn_rows(g - 1, 1 - i)
                if now:
                    product(g, i, 1)
                if before:
                    route(g - 1, 1 - i)
                for t in (2, 3):
                    half = (t - 2) * FC // 2
                    if now and after:
                        product(g, i, t, lambda c: spread_inverse(g + 1, 1 - i, half + c))
                    elif now:
                        product(g, i, t)
                    elif after:
                        for c in range(FC // 2):
                            spread_inverse(g + 1, 1 - i, half + c)

            run(pe, turn)

        @block.scalar
        def _(act):
            act.sem_inc(z_t_ready.sem, z_t_ready.start)
            act.sem_inc(exps_ready.sem, exps_ready.start)
            act.sem_inc(inv_hi.sem, inv_hi.start)
            act.wait_ge(set_up, 3)
            act.wait_ge(zeroed, 4)
            for n in range(2):
                cs = slice(n * FC // 2, (n + 1) * FC // 2)
                act.activation(spread[:, cs, :], spread_f[:, cs].rearrange("p c h n -> p c (h n)"),
                               ACT.Copy).then_inc(constants, 1)
            for i in range(PAR):
                act.activation(inv_r[i][:], zeros[:], ACT.Copy).then_inc(constants, 1)
            act.wait_ge(constants, 2 + PAR)
            def turn(g, i, k, now, after, before):
                if after:
                    act.wait_ge(inverted.sem, inverted.done(g + 1))
                    act.wait_ge(inv_spread.sem, inv_spread.done(g + 1 - PAR))
                    act.activation(inv_r[1 - i][0:HEADS, :], inv[1 - i][:], ACT.Copy).then_inc(inv_hi.sem, 1)
                if before:
                    for c in range(KC):
                        act.wait_ge(z_turned.sem, z_turned.done(g - 1, c + 1))
                        act.activation(z_t[1 - i][:, c, :], ps_z[c][:], ACT.Copy).then_inc(z_t_ready.sem, 1)
                    act.wait_ge(soft_step.sem, soft_step.done(g - 1, 3))
                    act.activation(exps[1 - i][:], logits[1 - i][:], ACT.Exp).then_inc(exps_ready.sem, 1)
                if now:
                    act.wait_ge(h_ready.sem, h_ready.done(g))
                    act.dma_start(h_rows[bass.ds(g * GRP, GRP), :].rearrange("(t p) n -> p t n", p=P),
                                  h_new[i][:]).then_inc(stored[i], 16)
                    act.wait_ge(z_ready.sem, z_ready.done(g))
                    act.dma_start(x_rows[bass.ds(g * GRP, GRP), :].rearrange("(t p) n -> p t n", p=P),
                                  z_hat[i][:]).then_inc(stored[i], 16)

            run(act, turn)


def build_choice(nc, probs, n_chosen, slot_ids, slot_gates):
    _, TILES, E = probs.shape
    HALF = TILES // 2
    assert HALF * E == P
    SC = n_chosen // P
    BITS = 30
    STEPS = BITS // 2
    INFO = 5
    with ExitStack() as ctx:
        def sb(name, shape, dt=F32):
            return ctx.enter_context(nc.sbuf_tensor(name, shape, dt))

        def psum(name, shape):
            return ctx.enter_context(nc.psum_tensor(name, shape, F32))

        def sem(name):
            return ctx.enter_context(nc.semaphore(name))

        ident = sb("ch_ident", [P, P])
        same = sb("ch_same", [P, P])
        earlier = sb("ch_earlier", [P, P])
        dist = sb("ch_dist", [P, P], I32)
        dist_mod = sb("ch_dist_mod", [P, P], I32)
        dist_f = sb("ch_dist_f", [P, P])
        ones = sb("ch_ones", [P, P])
        slots = sb("ch_slots", [P, P], F16)
        slot_cols = sb("ch_slot_cols", [P, TILES * E, SC])
        cand_bits = sb("ch_cand_bits", [P, STEPS, 3], I32)
        info = sb("ch_info", [P, TILES, E, INFO], BF16)
        rest = sb("ch_rest", [P, TILES, E])
        vals = sb("ch_vals", [P, 2, P])
        hit = [sb(f"ch_hit{k}", [P, 2, P]) for k in range(3)]
        thr = sb("ch_thr", [P, 1], I32)
        cand = sb("ch_cand", [P, 3], I32)
        counts = sb("ch_counts", [P, 3])
        met = sb("ch_met", [P, 3])
        digit = sb("ch_digit", [P, 1])
        digit_bits = sb("ch_digit_bits", [P, 1], I32)
        above = sb("ch_above", [P, 2, P])
        equal = sb("ch_equal", [P, 2, P])
        rank = sb("ch_rank", [P, 2, P])
        offset = sb("ch_offset", [P, 2])
        need = sb("ch_need", [P, 1])
        chosen = sb("ch_chosen", [P, 2, P])
        slot_of = sb("ch_slot_of", [P, TILES, E])
        slot_int = sb("ch_slot_int", [P, TILES, E], I32)
        slot_col_int = sb("ch_slot_col_int", [P, TILES, E], I32)
        slot_col = sb("ch_slot_col", [P, TILES, E])
        slot_row = sb("ch_slot_row", [P, TILES, E])
        slot_row_e = [sb(f"ch_slot_row_e{i}", [P, TILES]) for i in range(2)]
        in_col = sb("ch_in_col", [P, TILES * E, SC], BF16)
        info_col = sb("ch_info_col", [P, TILES, E, SC, INFO], BF16)
        hot = [sb(f"ch_hot{i}", [P, TILES, P], BF16) for i in range(2)]
        ids_f = sb("ch_ids_f", [P, E * SC])
        ps_t = [psum(f"ch_ps_t{i}", [P, P]) for i in range(2)]
        ps_c = psum("ch_ps_c", [P, 4])
        ps_i = psum("ch_ps_i", [P, E * SC, INFO])

        made = sem("ch_made")
        masks = sem("ch_masks")
        turned = sem("ch_turned")
        step_done = sem("ch_step_done")
        counted = sem("ch_counted")
        summed = sem("ch_summed")
        hot_ready = Steps(sem("ch_hot_ready"), TILES + 1)
        placed = Steps(sem("ch_placed"), 1)
        block = ctx.enter_context(nc.Block())

        @block.gpsimd
        def _(pool):
            pool.memset(ident[:], 0.0).then_inc(made, 1)
            pool.wait_ge(made, 1)
            pool.affine_select(out=ident[:], in_=ident[:], compare_op=ALU.not_equal, fill=1.0, base=0,
                               pattern=[[-1, P]], channel_multiplier=1).then_inc(masks, 1)
            pool.iota(dist[:], pattern=[[-1, P]], base=P, channel_multiplier=1).then_inc(made, 1)
            for s in range(STEPS):
                for k in range(3):
                    pool.memset(cand_bits[:, s, k:k + 1], (k + 1) << (BITS - 2 * s - 2)).then_inc(made, 1)
            pool.memset(ones[:], 1.0).then_inc(made, 1)
            pool.iota(slots[:], pattern=[[1, P]], base=0, channel_multiplier=0,
                      allow_small_or_imprecise_dtypes=True).then_inc(made, 1)
            pool.iota(slot_cols[:], pattern=[[0, TILES * E], [1, SC]], base=0, channel_multiplier=0,
                      allow_small_or_imprecise_dtypes=True).then_inc(made, 1)
            pool.iota(info[:, :, :, 0], pattern=[[0, TILES], [0, E]], base=0, channel_multiplier=1,
                      allow_small_or_imprecise_dtypes=True).then_inc(made, 1)
            pool.iota(info[:, :, :, 1], pattern=[[1, TILES], [0, E]], base=0, channel_multiplier=0,
                      allow_small_or_imprecise_dtypes=True).then_inc(made, 1)

        @block.vector
        def _(dve):
            n = [0]

            def then(instruction):
                n[0] += 1
                instruction.then_inc(step_done, 1)
                dve.wait_ge(step_done, n[0])

            dve.wait_ge(made, 2)
            then(dve.tensor_scalar(dist_mod[:], dist[:], E - 1, None, ALU.bitwise_and))
            then(dve.tensor_copy(dist_f[:], dist_mod[:]))
            then(dve.tensor_scalar(same[:], dist_f[:], 0.0, None, ALU.is_equal))
            then(dve.tensor_copy(dist_f[:], dist[:]))
            then(dve.scalar_tensor_tensor(out=earlier[:], in0=dist_f[:], scalar=float(P), in1=same[:],
                                          op0=ALU.is_lt, op1=ALU.mult))
            dve.wait_ge(made, 7 + 3 * STEPS)
            then(dve.tensor_copy(info[:, :, :, 2], probs[:]))
            then(dve.tensor_tensor(rest[:], probs[:], info[:, :, :, 2], ALU.subtract))
            then(dve.tensor_copy(info[:, :, :, 3], rest[:]))
            then(dve.tensor_tensor(rest[:], rest[:], info[:, :, :, 3], ALU.subtract))
            then(dve.tensor_copy(info[:, :, :, 4], rest[:]))
            dve.wait_ge(turned, 2)
            for i in range(2):
                then(dve.tensor_copy(vals[:, i, :], ps_t[i][:]))
            then(dve.memset(thr[:], 0))
            for s in range(STEPS):
                then(dve.tensor_tensor(cand[:], cand_bits[:, s, :], thr[:].broadcast_to([P, 3]), ALU.bitwise_or))
                for k in range(3):
                    dve.tensor_scalar(hit[k][:], vals[:], cand[:, k:k + 1].bitcast(F32), None, ALU.is_ge,
                                      ALU.add, accum_out=counts[:, k:k + 1]).then_inc(counted, 1)
                dve.wait_ge(summed, s + 1)
                then(dve.tensor_scalar(met[:], ps_c[:, 0:3], float(n_chosen), None, ALU.is_ge, ALU.add,
                                       accum_out=digit[:]))
                then(dve.tensor_scalar(digit_bits[:], digit[:], float(1 << (BITS - 2 * s - 2)), None, ALU.mult))
                then(dve.tensor_tensor(thr[:], thr[:], digit_bits[:], ALU.bitwise_or))
            thr_f = thr[:].bitcast(F32)
            then(dve.tensor_scalar(above[:], vals[:], thr_f, None, ALU.is_gt, ALU.add, accum_out=counts[:, 2:3]))
            then(dve.tensor_scalar(equal[:], vals[:], thr_f, None, ALU.is_equal))

            def ranks(flags, s):
                for i in range(2):
                    then(dve.tensor_tensor_scan(rank[:, i, :], ones[:], flags[:, i, :], 0.0, ALU.mult, ALU.add))
                then(dve.tensor_copy(counts[:, 0:2], rank[:, :, P - 1]))
                dve.sem_inc(counted, 3)
                dve.wait_ge(summed, s)
                then(dve.tensor_copy(offset[:], ps_c[:, 0:2]))
                for i in range(2):
                    then(dve.tensor_scalar(rank[:, i, :], rank[:, i, :], offset[:, i:i + 1], None, ALU.add))

            ranks(equal, STEPS + 1)
            then(dve.tensor_scalar(need[:], ps_c[:, 2:3], -1.0, float(n_chosen), ALU.mult, ALU.add))
            then(dve.tensor_scalar(rank[:], rank[:], need[:, 0:1], None, ALU.is_le))
            then(dve.tensor_tensor(equal[:], equal[:], rank[:], ALU.mult))
            then(dve.tensor_tensor(chosen[:], above[:], equal[:], ALU.add))
            ranks(chosen, STEPS + 2)
            then(dve.tensor_tensor(rank[:], rank[:], chosen[:], ALU.mult))
            then(dve.tensor_scalar(rank[:], rank[:], -1.0, None, ALU.add))
            dve.sem_inc(counted, 3)
            dve.wait_ge(turned, 4)
            for i in range(2):
                then(dve.tensor_copy(slot_of[:, i * HALF:(i + 1) * HALF, :].rearrange("p t e -> p (t e)"),
                                     ps_t[i][:]))
            then(dve.tensor_copy(slot_int[:], slot_of[:]))
            then(dve.tensor_scalar(slot_col_int[:], slot_int[:], P.bit_length() - 1, None, ALU.arith_shift_right))
            then(dve.tensor_scalar(slot_int[:], slot_int[:], P - 1, None, ALU.bitwise_and))
            then(dve.tensor_copy(slot_col[:], slot_col_int[:]))
            then(dve.tensor_copy(slot_row[:], slot_int[:]))
            then(dve.tensor_tensor(in_col[:], slot_cols[:], slot_col[:].rearrange("p t e -> p (t e)").unsqueeze(2)
                                   .broadcast_to([P, TILES * E, SC]), ALU.is_equal))
            for col in range(SC):
                then(dve.tensor_tensor(info_col[:, :, :, col, :].rearrange("p t e n -> p (t e) n"),
                                       info[:].rearrange("p t e n -> p (t e) n"),
                                       in_col[:, :, col:col + 1].broadcast_to([P, TILES * E, INFO]), ALU.mult))
            dve.sem_inc(hot_ready.sem, hot_ready.start)
            with dve.Fori(0, E // 2) as rnd:
                for i in range(2):
                    e = rnd * 2 + i
                    dve.wait_ge(placed.sem, placed.done(e - 2))
                    dve.tensor_copy(slot_row_e[i][:], slot_row[:, :, bass.ds(e, 1)]
                                    .rearrange("p t e -> p (t e)")).then_inc(hot_ready.sem, 1)
                    dve.wait_ge(hot_ready.sem, hot_ready.done(e, 1))
                    for t in range(TILES):
                        dve.tensor_scalar(hot[i][:, t, :], slots[:], slot_row_e[i][:, t:t + 1], None,
                                          ALU.is_equal).then_inc(hot_ready.sem, 1)
            dve.wait_ge(placed.sem, placed.done(E - 1))
            then(dve.tensor_copy(ids_f[:], ps_i[:, :, 0]))
            then(dve.scalar_tensor_tensor(out=ids_f[:], in0=ps_i[:, :, 1], scalar=float(P), in1=ids_f[:],
                                          op0=ALU.mult, op1=ALU.add))
            then(dve.tensor_copy(slot_ids[:].rearrange("p e s -> p (e s)"), ids_f[:]))
            gates = slot_gates[:].rearrange("p e s -> p (e s)")
            then(dve.tensor_copy(gates, ps_i[:, :, 4]))
            then(dve.tensor_tensor(gates, ps_i[:, :, 3], gates, ALU.add))
            then(dve.tensor_tensor(gates, ps_i[:, :, 2], gates, ALU.add))

        @block.tensor
        def _(pe):
            pe.wait_ge(masks, 1)
            flat = probs[:].rearrange("p t e -> p (t e)")
            for i in range(2):
                pe.transpose(ps_t[i][:], flat[:, i * P:(i + 1) * P], ident[:]).then_inc(turned, 1)
            for s in range(STEPS):
                pe.wait_ge(counted, 3 * (s + 1))
                pe.matmul(ps_c[:, 0:3], same[:], counts[:], start=True, stop=True).then_inc(summed, 1)
            for s in range(2):
                pe.wait_ge(counted, 3 * (STEPS + 1 + s))
                pe.matmul(ps_c[:, 0:1], earlier[:], counts[:, 0:1], start=True, stop=True)
                pe.matmul(ps_c[:, 1:2], earlier[:], counts[:, 1:2], start=True, stop=False)
                pe.matmul(ps_c[:, 1:2], same[:], counts[:, 0:1], start=False, stop=True)
                pe.matmul(ps_c[:, 2:3], same[:], counts[:, 2:3], start=True, stop=True).then_inc(summed, 1)
            pe.wait_ge(counted, 3 * (STEPS + 3))
            for i in range(2):
                pe.transpose(ps_t[i][:], rank[:, i, :], ident[:]).then_inc(turned, 1)
            pe.sem_inc(placed.sem, placed.start)
            with pe.Fori(0, E // 2) as rnd:
                for i in range(2):
                    e = rnd * 2 + i
                    for t in range(TILES):
                        pe.wait_ge(hot_ready.sem, hot_ready.done(e, t + 2))
                        mm = pe.matmul(ps_i[:, bass.ds(e * SC, SC), :].rearrange("p s n -> p (s n)"),
                                       hot[i][:, t, :],
                                       info_col[:, t, bass.ds(e, 1)].rearrange("p a s n -> p (a s n)"),
                                       start=(t == 0), stop=(t == TILES - 1))
                    mm.then_inc(placed.sem, 1)


def build_experts(nc, d, x_rows, slot_ids, slot_gates, out):
    _, E, SC = slot_ids.shape
    TOKENS, D = x_rows.shape
    KC = D // P
    FC = d["w_up"].shape[3] // P
    SLOTS = SC * P
    with ExitStack() as ctx:
        def sb(name, shape, dt=F32):
            return ctx.enter_context(nc.sbuf_tensor(name, shape, dt))

        def psum(name, shape):
            return ctx.enter_context(nc.psum_tensor(name, shape, F32))

        def sem(name):
            return ctx.enter_context(nc.semaphore(name))

        ident = sb("ex_ident", [P, P])
        w_up = [sb(f"ex_w_up{i}", [P, KC, FC * P]) for i in range(2)]
        b_up = [sb(f"ex_b_up{i}", [P, FC]) for i in range(2)]
        w_dn = [sb(f"ex_w_dn{i}", [P, FC, D]) for i in range(2)]
        b_dn = [sb(f"ex_b_dn{i}", [P, D]) for i in range(2)]
        ids_from = [sb(f"ex_ids_from{i}", [P, SC], I32) for i in range(2)]
        ids_to = [sb(f"ex_ids_to{i}", [P, SC], I32) for i in range(2)]
        gate = [sb(f"ex_gate{i}", [P, SC]) for i in range(2)]
        x = [sb(f"ex_x{i}", [P, SC, D]) for i in range(2)]
        w_up_hi = [sb(f"ex_w_up_hi{i}", [P, KC, FC * P], F32R) for i in range(2)]
        w_up_lo = [sb(f"ex_w_up_lo{i}", [P, KC, FC * P], F32R) for i in range(2)]
        w_dn_hi = [sb(f"ex_w_dn_hi{i}", [P, FC, D], F32R) for i in range(2)]
        w_dn_lo = [sb(f"ex_w_dn_lo{i}", [P, FC, D], F32R) for i in range(2)]
        x_hi = [sb(f"ex_x_hi{i}", [P, KC, SLOTS], F32R) for i in range(2)]
        x_lo = [sb(f"ex_x_lo{i}", [P, KC, SLOTS], F32R) for i in range(2)]
        mid = [sb(f"ex_mid{i}", [P, SLOTS]) for i in range(2)]
        mid_hi = sb("ex_mid_hi", [P, FC, SLOTS], F32R)
        mid_lo = sb("ex_mid_lo", [P, FC, SLOTS], F32R)
        y = [sb(f"ex_y{i}", [P, SC, D]) for i in range(2)]
        ps_x = [psum(f"ex_ps_x{k}", [P, SLOTS]) for k in range(KC)]
        ps_m = [psum(f"ex_ps_m{k}", [P, SLOTS]) for k in range(2)]
        ps_y = [psum(f"ex_ps_y{k}", [P, 2, D]) for k in range(SC // 2)]

        zeroed = sem("ex_zeroed")
        set_up = sem("ex_set_up")
        weights_in = [sem(f"ex_weights_in{i}") for i in range(2)]
        gathered = [sem(f"ex_gathered{i}") for i in range(2)]
        gather_begun = sem("ex_gather_begun")
        scatter_begun = sem("ex_scatter_begun")
        ids_from_ready = Steps(sem("ex_ids_from_ready"), 1)
        ids_to_ready = Steps(sem("ex_ids_to_ready"), 1)
        gates_ready = Steps(sem("ex_gates_ready"), 1)
        x_turned = Steps(sem("ex_x_turned"), KC)
        x_rounded = Steps(sem("ex_x_rounded"), KC)
        x_split = Steps(sem("ex_x_split"), KC)
        PER_K, PER_DN = 2, 2
        UP_PER, DN_PER = KC * PER_K, FC // PER_DN
        w_rounded = Steps(sem("ex_w_rounded"), UP_PER + DN_PER)
        w_split = Steps(sem("ex_w_split"), UP_PER + DN_PER)
        mid_full = Steps(sem("ex_mid_full"), FC)
        mid_ready = Steps(sem("ex_mid_ready"), 2 * FC)
        mid_split = Steps(sem("ex_mid_split"), FC)
        y_full = Steps(sem("ex_y_full"), SC // 2)
        y_step = Steps(sem("ex_y_step"), SC // 2)
        y_ready = Steps(sem("ex_y_ready"), SC)
        scattered = sem("ex_scattered")
        added = Steps(sem("ex_added"), 1)
        block = ctx.enter_context(nc.Block())

        def piece(i, n):
            if n < UP_PER:
                k, part, wide = n // PER_K, n % PER_K, FC * P // PER_K
                cs = slice(part * wide, (part + 1) * wide)
                return w_up[i][:, k, cs], w_up_hi[i][:, k, cs], w_up_lo[i][:, k, cs]
            cs = slice((n - UP_PER) * PER_DN, (n - UP_PER + 1) * PER_DN)
            return w_dn[i][:, cs, :], w_dn_hi[i][:, cs, :], w_dn_lo[i][:, cs, :]

        def run(eng, step):
            with eng.Fori(0, E // 2 - 1) as rnd:
                for i in range(2):
                    step(rnd * 2 + i, i, rnd, True)
            step(E - 2, 0, E // 2 - 1, True)
            step(E - 1, 1, E // 2 - 1, False)

        @block.sync
        def _(sp):
            with sp.Fori(0, E // 2) as rnd:
                for i in range(2):
                    e = rnd * 2 + i
                    sp.wait_ge(y_full.sem, y_full.done(e - 2))
                    sp.wait_ge(y_step.sem, y_step.done(e - 2))
                    one, grp = bass.ds(e, 1), bass.ds(rnd, 1)
                    sp.dma_start(w_up[i][:], d["w_up"][grp].rearrange("a p k n -> (a p) k n")).then_inc(weights_in[i], 16)
                    sp.dma_start(b_up[i][:], d["b_up"][grp].rearrange("a p k -> (a p) k")).then_inc(weights_in[i], 16)
                    sp.dma_start(w_dn[i][:], d["w_dn"][one].rearrange("a p k n -> (a p) k n")).then_inc(weights_in[i], 16)
                    sp.dma_start(b_dn[i][:], d["b_dn"][one].rearrange("a n -> (a n)")
                                 .partition_broadcast(P)).then_inc(weights_in[i], 16)

        @block.gpsimd
        def _(pool):
            pool.sem_inc(ids_from_ready.sem, ids_from_ready.start)
            pool.sem_inc(ids_to_ready.sem, ids_to_ready.start)
            pool.sem_inc(added.sem, added.start)
            pool.memset(ident[:], 0.0).then_inc(zeroed, 1)
            pool.wait_ge(zeroed, 1)
            pool.affine_select(out=ident[:], in_=ident[:], compare_op=ALU.not_equal, fill=1.0, base=0,
                               pattern=[[-1, P]], channel_multiplier=1).then_inc(set_up, 1)

            def gather(e, i):
                pool.wait_ge(x_turned.sem, x_turned.done(e - 2))
                pool.sem_inc(gather_begun, 1)
                pool.tensor_copy(ids_from[i][:].rearrange("p (a s) -> p a s", a=1),
                                 slot_ids[:, bass.ds(e, 1), :]).then_inc(ids_from_ready.sem, 1)
                pool.wait_ge(ids_from_ready.sem, ids_from_ready.done(e))
                pool.sem_inc(gather_begun, 1)
                for sc in range(SC):
                    pool.indirect_dma_start(
                        out=x[i][:, sc, :], out_offset=None, in_=x_rows,
                        in_offset=bass.IndirectOffsetOnAxis(ap=ids_from[i][:, sc:sc + 1], axis=0),
                    ).then_inc(gathered[i], 16)

            def scatter(e, i):
                pool.tensor_copy(ids_to[i][:].rearrange("p (a s) -> p a s", a=1),
                                 slot_ids[:, bass.ds(e, 1), :]).then_inc(ids_to_ready.sem, 1)
                pool.wait_ge(ids_to_ready.sem, ids_to_ready.done(e))
                pool.wait_ge(y_ready.sem, y_ready.done(e))
                pool.sem_inc(scatter_begun, 1)
                for sc in range(SC):
                    pool.indirect_dma_start(
                        out=out, out_offset=bass.IndirectOffsetOnAxis(ap=ids_to[i][:, sc:sc + 1], axis=0),
                        in_=y[i][:, sc, :], in_offset=None, compute_op=ALU.add,
                    ).then_inc(scattered, 16)
                pool.wait_ge(scattered, (e + 1) * (16 * SC))
                pool.sem_inc(added.sem, 1)

            gather(0, 0)
            gather(1, 1)
            with pool.Fori(0, E // 2 - 1) as rnd:
                for i in range(2):
                    e = rnd * 2 + i
                    gather(e + 2, i)
                    scatter(e, i)
            scatter(E - 2, 0)
            scatter(E - 1, 1)

        @block.vector
        def _(dve):
            for ev in (gates_ready, y_step, y_ready, x_split, w_split, mid_split):
                dve.sem_inc(ev.sem, ev.start)

            def split_weights(e, i, pieces):
                for n in pieces:
                    raw, hi, lo = piece(i, n)
                    dve.wait_ge(w_rounded.sem, w_rounded.done(e, n + 1))
                    dve.tensor_tensor(lo, raw, hi.bitcast(F32), ALU.subtract).then_inc(w_split.sem, 1)

            def split_rows(e, i):
                for k in range(KC):
                    dve.wait_ge(x_rounded.sem, x_rounded.done(e, k + 1))
                    dve.tensor_tensor(x_lo[i][:, k, :], ps_x[k][:], x_hi[i][:, k, :].bitcast(F32),
                                      ALU.subtract).then_inc(x_split.sem, 1)

            def step(e, i, rnd, more):
                dve.tensor_copy(gate[i][:].rearrange("p (a s) -> p a s", a=1),
                                slot_gates[:, bass.ds(e, 1), :]).then_inc(gates_ready.sem, 1)
                for c in range(FC):
                    dve.wait_ge(mid_ready.sem, mid_ready.done(e, 2 * (c + 1)))
                    dve.tensor_tensor(mid_lo[:, c, :], mid[c % 2][:], mid_hi[:, c, :].bitcast(F32),
                                      ALU.subtract).then_inc(mid_split.sem, 1)
                if more:
                    split_rows(e + 1, 1 - i)
                dve.wait_ge(gates_ready.sem, gates_ready.done(e))
                dve.wait_ge(added.sem, added.done(e - 2))
                for j in range(SC // 2):
                    if more:
                        split_weights(e + 1, 1 - i, range(UP_PER) if j == 0 else range(UP_PER, UP_PER + DN_PER))
                    dve.wait_ge(y_full.sem, y_full.done(e, j + 1))
                    dve.tensor_tensor(y[i][:, 2 * j:2 * j + 2, :], ps_y[j][:],
                                      b_dn[i][:].unsqueeze(1).broadcast_to([P, 2, D]),
                                      ALU.add).then_inc(y_step.sem, 1)
                    dve.wait_ge(y_step.sem, y_step.done(e, j + 1))
                    for sc in (2 * j, 2 * j + 1):
                        dve.tensor_scalar(y[i][:, sc, :], y[i][:, sc, :], gate[i][:, sc:sc + 1], None,
                                          ALU.mult).then_inc(y_ready.sem, 1)

            split_weights(0, 0, range(UP_PER + DN_PER))
            split_rows(0, 0)
            run(dve, step)

        @block.scalar
        def _(act):
            for ev in (x_rounded, w_rounded, mid_ready):
                act.sem_inc(ev.sem, ev.start)

            def round_weights(e, i, landed):
                act.wait_ge(weights_in[i], landed)
                act.wait_ge(y_full.sem, y_full.done(e - 2))
                for n in range(UP_PER + DN_PER):
                    raw, hi, _ = piece(i, n)
                    act.activation(hi, raw, ACT.Copy).then_inc(w_rounded.sem, 1)

            def round_rows(e, i):
                for k in range(KC):
                    act.wait_ge(x_turned.sem, x_turned.done(e, k + 1))
                    act.activation(x_hi[i][:, k, :], ps_x[k][:], ACT.Copy).then_inc(x_rounded.sem, 1)

            def step(e, i, rnd, more):
                for c in range(FC):
                    act.wait_ge(mid_full.sem, mid_full.done(e, c + 1))
                    act.wait_ge(mid_split.sem, mid_split.done(e, c - 1))
                    for out in (mid[c % 2][:], mid_hi[:, c, :]):
                        act.activation(out, ps_m[c % 2][:], ACT.Silu,
                                       bias=b_up[i][:, c:c + 1]).then_inc(mid_ready.sem, 1)
                if more:
                    round_rows(e + 1, 1 - i)
                    round_weights(e + 1, 1 - i, (rnd + 1 + i) * 64)

            round_weights(0, 0, 64)
            round_rows(0, 0)
            run(act, step)

        @block.tensor
        def _(pe):
            for ev in (x_turned, mid_full, y_full):
                pe.sem_inc(ev.sem, ev.start)
            pe.wait_ge(set_up, 1)

            def product(out, hi, lo, by_hi, by_lo, first, last):
                pe.matmul(out, hi, by_hi, start=first, stop=False)
                pe.matmul(out, hi, by_lo, start=False, stop=False)
                return pe.matmul(out, lo, by_hi, start=False, stop=last)

            def turn(e, i, landed):
                pe.wait_ge(gathered[i], landed)
                pe.wait_ge(x_split.sem, x_split.done(e - 1))
                for k in range(KC):
                    for sc in range(SC):
                        mm = pe.transpose(ps_x[k][:, sc * P:(sc + 1) * P], x[i][:, sc, k * P:(k + 1) * P], ident[:])
                    mm.then_inc(x_turned.sem, 1)

            def up(e, i):
                pe.wait_ge(w_split.sem, w_split.done(e, UP_PER))
                pe.wait_ge(x_split.sem, x_split.done(e))
                for c in range(FC):
                    pe.wait_ge(mid_ready.sem, mid_ready.done(e, 2 * (c - 1)))
                    cs = slice(c * P, (c + 1) * P)
                    for k in range(KC):
                        mm = product(ps_m[c % 2][:], w_up_hi[i][:, k, cs], w_up_lo[i][:, k, cs],
                                     x_hi[i][:, k, :], x_lo[i][:, k, :], k == 0, k == KC - 1)
                    mm.then_inc(mid_full.sem, 1)

            def down(e, i):
                pe.wait_ge(w_split.sem, w_split.done(e))
                for j in range(SC // 2):
                    pe.wait_ge(y_step.sem, y_step.done(e - 1, j + 1))
                    for sc in (2 * j, 2 * j + 1):
                        cs = slice(sc * P, (sc + 1) * P)
                        for c in range(FC):
                            if sc == 0:
                                pe.wait_ge(mid_split.sem, mid_split.done(e, c + 1))
                            mm = product(ps_y[j][:, sc % 2, :], mid_hi[:, c, cs], mid_lo[:, c, cs],
                                         w_dn_hi[i][:, c, :], w_dn_lo[i][:, c, :], c == 0, c == FC - 1)
                    mm.then_inc(y_full.sem, 1)

            def step(e, i, rnd, more):
                up(e, i)
                if more:
                    turn(e + 1, 1 - i, (rnd + 1 + i) * (16 * SC))
                down(e, i)

            turn(0, 0, 16 * SC)
            run(pe, step)


def build(nc, d, out):
    TOKENS, D = out.shape
    E = d["w_dn"].shape[0]
    HEADS_HD = d["w_q"].shape[0] * P
    h_mixed = nc.dram_tensor("h_mixed", [TOKENS, D], F32, kind="Internal").ap()
    sums = nc.dram_tensor("attention_sums", [HEADS_HD // (P // 2), TOKENS], F32, kind="Internal").ap()
    o_t = nc.dram_tensor("attention_t", [HEADS_HD, TOKENS], F32, kind="Internal").ap()
    x_rows = nc.dram_tensor("x_rows", [TOKENS, D], F32, kind="Internal").ap()
    build_token_mixer(nc, d, h_mixed)
    with ExitStack() as ctx:
        x_t = ctx.enter_context(nc.sbuf_tensor("x_t", [P, D // P, TOKENS], F32))
        c_t = ctx.enter_context(nc.sbuf_tensor("c_t", [P, TOKENS], F32))
        build_latent(nc, d, h_mixed, x_t, c_t)
        build_attention(nc, d, x_t, c_t, o_t, sums)
    with ExitStack() as ctx:
        probs = ctx.enter_context(nc.sbuf_tensor("probs", [P, TOKENS // P, E], F32))
        slot_ids = ctx.enter_context(nc.sbuf_tensor("slot_ids", [P, E, TOKENS // E // P], I32))
        slot_gates = ctx.enter_context(nc.sbuf_tensor("slot_gates", [P, E, TOKENS // E // P], F32))
        build_router(nc, d, o_t, sums, h_mixed, out, x_rows, probs)
        build_choice(nc, probs, TOKENS // E, slot_ids, slot_gates)
        build_experts(nc, d, x_rows, slot_ids, slot_gates, out)


def _layout(i):
    import numpy as np

    a = {k.replace("L0_", ""): np.asarray(v) for k, v in i.items()}

    def stationary(w):
        L, F, K = w.shape
        return w.transpose(2, 0, 1).reshape(K // P, P, L, F).transpose(1, 2, 0, 3)

    def columns(v):
        L, F = v.shape
        return v.reshape(L, F // P, P).transpose(2, 0, 1)

    L, F = a["tok_conv_b"].shape
    B = a["x"].shape[0]
    D = a["tok_tok_emb"].shape[1]
    kv = a["attn_w_kv_up"]
    wide = kv.shape[1] // 2
    pairs = wide // P
    NG, _, FF = a["ffn_W_up"].shape
    E = a["ffn_W_down"].shape[0]
    pad = -FF % P
    o = {
        "x": a["x"].reshape(B, -1, P).transpose(2, 0, 1),
        "tok_emb": a["tok_tok_emb"],
        "pos_emb": a["tok_pos_emb"],
        "w_in": stationary(a["tok_W_in"]),
        "w_b": stationary(a["tok_W_B"]),
        "w_out": stationary(a["tok_W_out"]),
        "w_c": a["tok_W_C"].transpose(2, 0, 1),
        "conv_w": a["tok_conv_w"].reshape(L, F // P, P, -1).transpose(2, 0, 1, 3),
        "conv_b": columns(a["tok_conv_b"]),
        "d_vec": columns(a["tok_D_vec"]),
        "g_col": columns(a["tok_ln_g"]),
        "b_col": columns(a["tok_ln_b"]),
        "ln_g": a["tok_ln_g"],
        "ln_b": a["tok_ln_b"],
        "w_kv_down": a["attn_w_kv_down"],
        "w_q": a["attn_w_q"].reshape(D // P, P, pairs, P).transpose(2, 1, 0, 3),
        "w_k": kv[:, :wide].reshape(P, pairs, P).transpose(1, 0, 2),
        "w_v": kv[:, wide:].reshape(P, pairs, P).transpose(1, 0, 2),
        "w_o": a["attn_w_out"],
        "w_r": a["ffn_Wr"].reshape(D // P, P, E).transpose(1, 0, 2),
        "b_r": a["ffn_br"],
        "w_up": np.pad(a["ffn_W_up"], ((0, 0), (0, 0), (0, pad))).reshape(NG, D // P, P, -1).transpose(0, 2, 1, 3),
        "b_up": np.pad(a["ffn_b_up"], ((0, 0), (0, pad))).reshape(NG, -1, P).transpose(0, 2, 1),
        "w_dn": np.pad(a["ffn_W_down"], ((0, 0), (0, pad), (0, 0))).reshape(E, -1, P, D).transpose(0, 2, 1, 3),
        "b_dn": a["ffn_b_down"],
    }
    return {k: np.ascontiguousarray(v) for k, v in o.items()}


def kernel(**inputs):
    import numpy as _np
    import concourse.bacc as _bacc
    from concourse import mybir as _mybir
    from concourse.bass_utils import run_bass_kernel_spmd as _run

    nc = _bacc.Bacc("TRN2", target_bir_lowering=False, num_devices=1)
    arrays, d = {}, {}
    for name, a in _layout(inputs).items():
        arrays[f"in_{name}"] = a
        d[name] = nc.dram_tensor(f"in_{name}", a.shape, _mybir.dt.from_np(a.dtype), kind="ExternalInput").ap()
    b, t = inputs["x"].shape
    dim = inputs["L0_tok_tok_emb"].shape[1]
    out = nc.dram_tensor("out_0", (b * t, dim), _mybir.dt.float32, kind="ExternalOutput").ap()
    build(nc, d, out)
    r = _run(nc, [arrays], core_ids=[0])
    return r.results[0]["out_0"].reshape(b, t, dim)
```
